# Optimizing a Trainium2 kernel written in Bass

```python
import numpy as np
import jax
import jax.numpy as jnp

def _softmax(x, axis=-1):
    return jax.nn.softmax(x, axis=axis)

def _gelu(x):
    return jax.nn.gelu(x, approximate=True)

def _silu(x):
    return jax.nn.silu(x)

def _sigmoid(x):
    return jax.nn.sigmoid(x)

def _layernorm(x, axis=-1, eps=1e-05):
    m = jnp.mean(x, axis=axis, keepdims=True)
    v = jnp.var(x, axis=axis, keepdims=True)
    return (x - m) / jnp.sqrt(v + eps)

def _scatter_add(tgt, idx, src, axis=0):
    return tgt.at[idx].add(src)

def _segment_sum(src, seg, n):
    return jax.ops.segment_sum(src, seg, n)
kernel_name = 'mk_hybrid_d1_jaxref_r8_b0eea7'

def setup_inputs(seed: int=0):
    np.random.seed(seed)
    _w = jnp.asarray

    def _L0_attn_a_setup():
        import jax, jax.numpy as jnp
        import numpy as np
        B, S, D = (4, 512, 128)
        GROUP = 32
        HEAD = 128
        INNER = 256
        key = jax.random.key(seed)
        ks = jax.random.split(key, 16)
        s = 0.02
        return {'x': jax.random.normal(ks[0], (B, S, D), jnp.float32), 'Wv': jax.random.normal(ks[1], (D, INNER), jnp.float32) * s, 'bv': jnp.zeros((INNER,), jnp.float32), 'Wg': jax.random.normal(ks[2], (D, INNER), jnp.float32) * s, 'bg': jnp.zeros((INNER,), jnp.float32), 'Win': jax.random.normal(ks[3], (D, HEAD), jnp.float32) * s, 'bin_': jnp.zeros((HEAD,), jnp.float32), 'Wout': jax.random.normal(ks[4], (INNER, D), jnp.float32) * s, 'bout': jnp.zeros((D,), jnp.float32), 'g_qq': 1.0 + jax.random.normal(ks[5], (HEAD,), jnp.float32) * s, 'b_qq': jnp.zeros((HEAD,), jnp.float32), 'g_qk': 1.0 + jax.random.normal(ks[6], (HEAD,), jnp.float32) * s, 'b_qk': jnp.zeros((HEAD,), jnp.float32), 'g_lq': 1.0 + jax.random.normal(ks[7], (HEAD,), jnp.float32) * s, 'b_lq': jnp.zeros((HEAD,), jnp.float32), 'g_lk': 1.0 + jax.random.normal(ks[8], (HEAD,), jnp.float32) * s, 'b_lk': jnp.zeros((HEAD,), jnp.float32)}
    _L0_attn_a_in = _L0_attn_a_setup()

    def _L0_attn_b_setup():
        import jax, jax.numpy as jnp
        import numpy as np
        B, S, D = (2, 256, 128)
        H, P = (16, 64)
        NUM_OUT = 128
        key = jax.random.key(seed)
        ks = jax.random.split(key, 9)
        sc = 0.05
        return {'x': jax.random.normal(ks[0], (B, S, D), jnp.float32), 'q_w': jax.random.normal(ks[1], (H, P, D), jnp.float32) * sc, 'q_b': jax.random.normal(ks[2], (H, 1, P), jnp.float32) * sc, 'k_w': jax.random.normal(ks[3], (H, P, D), jnp.float32) * sc, 'k_b': jax.random.normal(ks[4], (H, 1, P), jnp.float32) * sc, 'v_w': jax.random.normal(ks[5], (H, P, D), jnp.float32) * sc, 'v_b': jax.random.normal(ks[6], (H, 1, P), jnp.float32) * sc, 'l_w': jax.random.normal(ks[7], (NUM_OUT, P * H), jnp.float32) * sc, 'l_b': jax.random.normal(ks[8], (1, NUM_OUT), jnp.float32) * sc}
    _L0_attn_b_in = _L0_attn_b_setup()

    def _L0_ffn_setup():
        import jax, jax.numpy as jnp
        import numpy as np
        K = 2
        CAP_FACTOR = 1.25
        key = jax.random.key(seed)
        ks = jax.random.split(key, 6)
        B, T, C, H, E = (8, 256, 128, 512, 8)
        return {'x': jax.random.normal(ks[0], (B, T, C), dtype=jnp.float32), 'Wr': jax.random.normal(ks[1], (C, E), dtype=jnp.float32) * 0.02, 'W1': jax.random.normal(ks[2], (E, C, H), dtype=jnp.float32) * 0.02, 'b1': jax.random.normal(ks[3], (E, H), dtype=jnp.float32) * 0.02, 'W2': jax.random.normal(ks[4], (E, H, C), dtype=jnp.float32) * 0.02, 'b2': jax.random.normal(ks[5], (E, C), dtype=jnp.float32) * 0.02}
    _L0_ffn_in = _L0_ffn_setup()
    _d = {'L0_attn_a_x': _L0_attn_a_in['x'], 'L0_attn_a_Wv': _L0_attn_a_in['Wv'], 'L0_attn_a_bv': _L0_attn_a_in['bv'], 'L0_attn_a_Wg': _L0_attn_a_in['Wg'], 'L0_attn_a_bg': _L0_attn_a_in['bg'], 'L0_attn_a_Win': _L0_attn_a_in['Win'], 'L0_attn_a_bin_': _L0_attn_a_in['bin_'], 'L0_attn_a_Wout': _L0_attn_a_in['Wout'], 'L0_attn_a_bout': _L0_attn_a_in['bout'], 'L0_attn_a_g_qq': _L0_attn_a_in['g_qq'], 'L0_attn_a_b_qq': _L0_attn_a_in['b_qq'], 'L0_attn_a_g_qk': _L0_attn_a_in['g_qk'], 'L0_attn_a_b_qk': _L0_attn_a_in['b_qk'], 'L0_attn_a_g_lq': _L0_attn_a_in['g_lq'], 'L0_attn_a_b_lq': _L0_attn_a_in['b_lq'], 'L0_attn_a_g_lk': _L0_attn_a_in['g_lk'], 'L0_attn_a_b_lk': _L0_attn_a_in['b_lk'], 'L0_attn_b_q_w': _L0_attn_b_in['q_w'], 'L0_attn_b_q_b': _L0_attn_b_in['q_b'], 'L0_attn_b_k_w': _L0_attn_b_in['k_w'], 'L0_attn_b_k_b': _L0_attn_b_in['k_b'], 'L0_attn_b_v_w': _L0_attn_b_in['v_w'], 'L0_attn_b_v_b': _L0_attn_b_in['v_b'], 'L0_attn_b_l_w': _L0_attn_b_in['l_w'], 'L0_attn_b_l_b': _L0_attn_b_in['l_b'], 'L0_ffn_Wr': _L0_ffn_in['Wr'], 'L0_ffn_W1': _L0_ffn_in['W1'], 'L0_ffn_b1': _L0_ffn_in['b1'], 'L0_ffn_W2': _L0_ffn_in['W2'], 'L0_ffn_b2': _L0_ffn_in['b2']}
    _x0 = _d['L0_attn_a_x']
    _d['L0_attn_a_x'] = jax.random.normal(jax.random.fold_in(jax.random.key(seed), 1), (4, 1024, 128), dtype=_x0.dtype)
    del _x0
    return _d

def reference(L0_attn_a_x, L0_attn_a_Wv, L0_attn_a_bv, L0_attn_a_Wg, L0_attn_a_bg, L0_attn_a_Win, L0_attn_a_bin_, L0_attn_a_Wout, L0_attn_a_bout, L0_attn_a_g_qq, L0_attn_a_b_qq, L0_attn_a_g_qk, L0_attn_a_b_qk, L0_attn_a_g_lq, L0_attn_a_b_lq, L0_attn_a_g_lk, L0_attn_a_b_lk, L0_attn_b_q_w, L0_attn_b_q_b, L0_attn_b_k_w, L0_attn_b_k_b, L0_attn_b_v_w, L0_attn_b_v_b, L0_attn_b_l_w, L0_attn_b_l_b, L0_ffn_Wr, L0_ffn_W1, L0_ffn_b1, L0_ffn_W2, L0_ffn_b2):

    def _L0_attn_a_ref(x, Wv, bv, Wg, bg, Win, bin_, Wout, bout, g_qq, b_qq, g_qk, b_qk, g_lq, b_lq, g_lk, b_lk):
        import jax, jax.numpy as jnp
        import numpy as np
        B, S, D = (4, 512, 128)
        GROUP = 32
        HEAD = 128
        INNER = 256
        b, s, d = x.shape
        g = s // GROUP
        xc = x.reshape(b, g, GROUP, d)
        v = jax.nn.silu(xc @ Wv + bv)
        gate = jax.nn.silu(xc @ Wg + bg)
        x_ = jax.nn.silu(xc @ Win + bin_)
        quad_q = x_ * g_qq + b_qq
        quad_k = x_ * g_qk + b_qk
        lin_q = x_ * g_lq + b_lq
        lin_k = x_ * g_lk + b_lk
        scale = jnp.asarray(INNER ** 0.5, x.dtype)
        attn = jnp.einsum('bgns,bgms->bgnm', quad_q, quad_k) / scale
        causal_mask = jnp.triu(jnp.ones((GROUP, GROUP), bool), 1)
        attn = jnp.where(causal_mask, 0.0, attn)
        attn = jnp.square(jax.nn.relu(attn))
        v_quad = jnp.einsum('bgnm,bgme->bgne', attn, v)
        kv = jnp.einsum('bgcs,bgce->bgse', lin_k, v)
        kv = jnp.cumsum(kv, axis=1) - kv
        v_lin = jnp.einsum('bgcs,bgse->bgce', lin_q, kv)
        o = (v_quad + v_lin) * gate
        o = o @ Wout + bout
        return o.reshape(b, s, d)

    def _L0_attn_b_ref(x, q_w, q_b, k_w, k_b, v_w, v_b, l_w, l_b):
        import jax, jax.numpy as jnp
        import numpy as np
        B, S, D = (2, 256, 128)
        H, P = (16, 64)
        NUM_OUT = 128
        q = jnp.einsum('bsd,hpd->bhsp', x, q_w) + q_b
        k = jnp.einsum('bsd,hpd->bhsp', x, k_w) + k_b
        v = jnp.einsum('bsd,hpd->bhsp', x, v_w) + v_b
        scores = jnp.einsum('bhqp,bhkp->bhqk', q, k) / jnp.sqrt(jnp.float32(P))
        attn = jax.nn.softmax(scores, axis=2)
        ctx = jnp.einsum('bhqk,bhkp->bqhp', attn, v)
        concat = ctx.reshape(ctx.shape[0], ctx.shape[1], H * P)
        out = concat @ l_w.T + l_b
        return out

    def _L0_ffn_ref(x, Wr, W1, b1, W2, b2):
        import jax, jax.numpy as jnp
        import numpy as np
        K = 2
        CAP_FACTOR = 1.25
        B, T, C = x.shape
        E = Wr.shape[1]
        capacity = int(T / E * CAP_FACTOR)
        probs = jax.nn.softmax(x @ Wr, axis=-1)
        topk_probs, topk_experts = jax.lax.top_k(probs, K)
        S = T * K
        e_flat = topk_experts.reshape(B, S)
        p_flat = topk_probs.reshape(B, S)
        x_rep = jnp.repeat(x, K, axis=1)
        onehot = jax.nn.one_hot(e_flat, E, dtype=jnp.int32)
        pos_all = jnp.cumsum(onehot, axis=1) - onehot
        pos = jnp.take_along_axis(pos_all, e_flat[..., None], axis=-1)[..., 0]
        keep = pos < capacity
        pos_c = jnp.minimum(pos, capacity - 1)
        b_idx = jnp.broadcast_to(jnp.arange(B)[:, None], (B, S))
        buf = jnp.zeros((E, B, capacity, C), dtype=x.dtype)
        buf = buf.at[e_flat, b_idx, pos_c].add(x_rep * keep[..., None].astype(x.dtype))
        h = jax.nn.relu(jnp.einsum('ebnc,ech->ebnh', buf, W1) + b1[:, None, None, :])
        y = jnp.einsum('ebnh,ehc->ebnc', h, W2) + b2[:, None, None, :]
        y_tok = y[e_flat, b_idx, pos_c]
        y_tok = y_tok * keep[..., None].astype(x.dtype) * p_flat[..., None]
        out = y_tok.reshape(B, T, K, C).sum(axis=2)
        return out
    x = L0_attn_a_x
    x = x + _L0_attn_a_ref(_layernorm(x, axis=-1), L0_attn_a_Wv, L0_attn_a_bv, L0_attn_a_Wg, L0_attn_a_bg, L0_attn_a_Win, L0_attn_a_bin_, L0_attn_a_Wout, L0_attn_a_bout, L0_attn_a_g_qq, L0_attn_a_b_qq, L0_attn_a_g_qk, L0_attn_a_b_qk, L0_attn_a_g_lq, L0_attn_a_b_lq, L0_attn_a_g_lk, L0_attn_a_b_lk)
    x = x + _L0_ffn_ref(_layernorm(x, axis=-1), L0_ffn_Wr, L0_ffn_W1, L0_ffn_b1, L0_ffn_W2, L0_ffn_b2)
    x = x + _L0_attn_b_ref(_layernorm(x, axis=-1), L0_attn_b_q_w, L0_attn_b_q_b, L0_attn_b_k_w, L0_attn_b_k_b, L0_attn_b_v_w, L0_attn_b_v_b, L0_attn_b_l_w, L0_attn_b_l_b)
    x = x + _L0_ffn_ref(_layernorm(x, axis=-1), L0_ffn_Wr, L0_ffn_W1, L0_ffn_b1, L0_ffn_W2, L0_ffn_b2)
    return x

_drawn_inputs = setup_inputs


def setup_inputs(seed=0):
    import zlib

    import numpy as np

    out = dict(_drawn_inputs(seed))
    spreads = {'L0_attn_a_bv': (0.0, 0.1),
     'L0_attn_a_bg': (0.0, 0.1),
     'L0_attn_a_bin_': (0.0, 0.1),
     'L0_attn_a_bout': (0.0, 0.1),
     'L0_attn_a_b_qq': (0.0, 0.1),
     'L0_attn_a_b_qk': (0.0, 0.1),
     'L0_attn_a_b_lq': (0.0, 0.1),
     'L0_attn_a_b_lk': (0.0, 0.1)}
    factors = {}
    for name, (base, spread) in spreads.items():
        noise = np.random.default_rng([zlib.crc32(name.encode()), seed]).standard_normal(out[name].shape)
        drawn = base * np.exp(spread * noise) if base else spread * noise
        out[name] = jnp.asarray(drawn.astype(out[name].dtype))
    for name, factor in factors.items():
        out[name] = (out[name] * factor).astype(out[name].dtype)
    return out
```

```python
from contextlib import ExitStack

import concourse.bass as bass
from concourse import mybir

F32 = mybir.dt.float32
F32R = mybir.dt.float32r
BF16 = mybir.dt.bfloat16
U32 = mybir.dt.uint32
ALU = mybir.AluOpType
ACT = mybir.ActivationFunctionType
X_AXIS = mybir.AxisListType.X

P = 128
B = 4
S = 1024
T = S // P
HALF = 512
GROUP = 32
INNER = 256
EH = INNER // P
E = 8
CAP = int(S / E * 1.25)
HID = 512
HC = HID // P
SLOTS = E * CAP
ST = SLOTS // P
HEADS = 16
HD = 64
PAIRS = HEADS // 2
EPS = 1e-5
SKIPPED = float(4 * B * SLOTS)
WQ, WK, WV, BQ, BK, BV, WCOLS = 0, P, 2 * P, 3 * P, 3 * P + 1, 3 * P + 2, 4 * P + 2


def bass_hybrid(nc, x, wv, bv, wg, win, wout, bout, cols_a, wr, w1, b1, w2, b2, wqkv, bqk, bvv, wl, bl, out):
    with ExitStack() as keep:
        def sb(name, shape, dt=F32, stack=keep):
            return stack.enter_context(nc.sbuf_tensor(name, shape, dt))

        def sem(name):
            return keep.enter_context(nc.semaphore(name))

        bank = keep.enter_context(nc.psum_tensor("bank", [P, 8, HALF], F32))
        xres = sb("xres", [P, B * T, P])
        xhat = sb("xhat", [P, T, P])
        xT = sb("xT", [P, S])
        ident = sb("ident", [P, P])
        stats = sb("stats", [P, T, 6])
        meanvar = sb("meanvar", [P, T, 2])
        rstd = sb("rstd", [P, T])
        varp = sb("varp", [P, T])
        minus_half = sb("minus_half", [P, T])
        w1_sb = sb("w1_sb", [P, E, HID])
        w2_sb = sb("w2_sb", [P, E, HC, P])
        b1_sb = sb("b1_sb", [P, E * HC])
        b2_sb = sb("b2_sb", [P, E])
        wr_sb = sb("wr_sb", [P, E])
        before = sb("before", [P, P], BF16)
        ones = sb("ones", [P, P], BF16)
        rev = sb("rev", [P, E])
        rowbase = sb("rowbase", [P, B, E])
        bl_sb = sb("bl_sb", [P, P])
        bout_sb = sb("bout_sb", [P, P])
        xslots = nc.dram_tensor("xslots", [B * SLOTS, P], F32, kind="Internal").ap()
        yslots = nc.dram_tensor("yslots", [B * SLOTS, P], F32, kind="Internal").ap()

        load_sem = sem("load_sem")
        load_c = sem("load_c")
        consts = sem("consts")
        pool_step = sem("pool_step")
        dve_step = sem("dve_step")
        zeroed = sem("zeroed")
        ln_stats = sem("ln_stats")
        ln_rstd = sem("ln_rstd")
        ln_xhat = sem("ln_xhat")
        ln_tr = sem("ln_tr")
        ln_xT = sem("ln_xT")
        biased = sem("biased")
        a_xproj, a_gproj, a_vproj, a_lktr = sem("a_xproj"), sem("a_gproj"), sem("a_vproj"), sem("a_lktr")
        a_sq, a_sl, a_kv, a_o, a_out = sem("a_sq"), sem("a_sl"), sem("a_kv"), sem("a_o"), sem("a_out")
        a_xs, a_gs, a_v, a_lkt, a_usq = sem("a_xs"), sem("a_gs"), sem("a_v"), sem("a_lkt"), sem("a_usq")
        a_feat, a_vbias, a_u, a_at = sem("a_feat"), sem("a_vbias"), sem("a_u"), sem("a_at")
        a_state, a_gated, a_res = sem("a_state"), sem("a_gated"), sem("a_res")
        f_lg, f_pos, f_str, f_h, f_y, f_ytr = (sem(n) for n in ("f_lg", "f_pos", "f_str", "f_h", "f_y", "f_ytr"))
        f_sub, f_exp, f_m, f_idx = sem("f_sub"), sem("f_exp"), sem("f_m"), sem("f_idx")
        f_xs, f_ha, f_hd, f_ya, f_ys = (sem(n) for n in ("f_xs", "f_ha", "f_hd", "f_ya", "f_ys"))
        f_sc, f_ld, f_st, f_ga, f_comb = (sem(n) for n in ("f_sc", "f_ld", "f_st", "f_ga", "f_comb"))
        c_stage, c_proj, c_hi, c_pev, c_dup = (sem(n) for n in ("c_stage", "c_proj", "c_hi", "c_pev", "c_dup"))
        c_qk, c_max, c_exp, c_vs, c_av = (sem(n) for n in ("c_qk", "c_max", "c_exp", "c_vs", "c_av"))
        c_ctx, c_out, c_res = sem("c_ctx"), sem("c_out"), sem("c_res")
        stored = sem("stored")
        waits = sem("waits")

        def hold(engine, s, value):
            engine.wait_ge(s, value)
            engine.sem_inc(waits, 1)

        class Steps:
            def __init__(self, engine, s):
                self.engine, self.sem, self.n = engine, s, 0

            def wait(self):
                self.engine.wait_ge(self.sem, self.n)

            def done(self, ins):
                self.n = self.n + 1
                ins.then_inc(self.sem, 1)

            def then(self, ins):
                self.done(ins)
                self.wait()

        per_row = {
            ln_stats: 1, ln_rstd: 1, ln_xhat: T, ln_tr: T, ln_xT: 2,
            a_xproj: 2, a_gproj: 4, a_vproj: T, a_lktr: T, a_sq: T, a_sl: T, a_kv: T - 1, a_o: 2 * T, a_out: T,
            a_xs: 2, a_gs: 4, a_v: 4, a_lkt: 2, a_usq: 2, a_feat: 4, a_vbias: 4, a_u: 2, a_at: 2, a_state: T - 1,
            a_gated: 4, a_res: 2,
            f_lg: 1, f_pos: 1, f_str: ST, f_h: 2 * E, f_y: E, f_ytr: ST, f_sub: 1, f_exp: 1, f_m: 1, f_idx: 1,
            f_xs: 3, f_ha: E, f_hd: E, f_ya: E, f_ys: 3, f_ld: 16, f_st: 16, f_comb: 2 * T,
            c_stage: PAIRS, c_proj: 6 * PAIRS, c_hi: 8 * PAIRS, c_pev: 6 * PAIRS, c_dup: 32 * PAIRS,
            c_qk: 2 * T * PAIRS, c_max: 2 * T * PAIRS, c_exp: 2 * T * PAIRS, c_vs: T * PAIRS, c_av: T * PAIRS,
            c_ctx: 2 * PAIRS, c_out: T, c_res: 2,
        }

        def ln_vector(v, step, n, b):
            for t in range(T):
                step.done(nc.vector.bn_stats(stats[:, t, :], xres[:, bass.ds(b * T + t, 1), :].rearrange("p a c -> p (a c)")))
            hold(v, dve_step, step.n)
            for t in range(T):
                ins = nc.vector.bn_aggr(meanvar[:, t, :], stats[:, t, :])
            ins.then_inc(ln_stats, 1)
            v.wait_ge(ln_rstd, n + 1)
            v.wait_ge(ln_tr, n * T)
            for t in range(T):
                nc.vector.tensor_scalar(xhat[:, t, :], xres[:, bass.ds(b * T + t, 1), :].rearrange("p a c -> p (a c)"),
                                        meanvar[:, t, 0:1], rstd[:, t:t + 1], ALU.subtract, ALU.mult).then_inc(ln_xhat, 1)

        def ln_pool(p, step, n, b, bias=None):
            hold(p, ln_stats, n + 1)
            step.then(nc.gpsimd.tensor_scalar(varp[:], meanvar[:, :, 1], EPS, None, ALU.add))
            nc.gpsimd.tensor_tensor(rstd[:], varp[:], minus_half[:], ALU.pow).then_inc(ln_rstd, 1)
            if bias is not None:
                hold(p, ln_xhat, (n + 1) * T)
                nc.gpsimd.tensor_tensor(xres[:, bass.ds(b * T, T), :], xres[:, bass.ds(b * T, T), :],
                                        bias[:].unsqueeze(1).to_broadcast([P, T, P]), ALU.add).then_inc(biased, 1)

        def ln_tensor(pe, n):
            for t in range(T):
                pe.wait_ge(ln_xhat, n * T + t + 1)
                nc.tensor.transpose(bank[:, t // 4, (t % 4) * P:(t % 4 + 1) * P], xhat[:, t, :], ident[:]).then_inc(ln_tr, 1)

        def ln_scalar(a, n):
            for h in range(2):
                a.wait_ge(ln_tr, n * T + 4 * (h + 1))
                nc.scalar.activation(xT[:, h * HALF:(h + 1) * HALF], bank[:, h, :], ACT.Copy).then_inc(ln_xT, 1)

        stage_a = ExitStack()
        wv_sb = sb("wv_sb", [P, INNER], stack=stage_a)
        wg_sb = sb("wg_sb", [P, INNER], stack=stage_a)
        win_sb = sb("win_sb", [P, P], stack=stage_a)
        wout_sb = sb("wout_sb", [P, EH, P], stack=stage_a)
        bv_sb = sb("bv_sb", [P, INNER], stack=stage_a)
        ca = sb("ca", [P, 11], stack=stage_a)
        m_quad = sb("m_quad", [P, P], stack=stage_a)
        m_lin = sb("m_lin", [P, P], stack=stage_a)
        base = sb("base", [P, S], stack=stage_a)
        qqT, qkT, lqT, lkT = (sb(n, [P, S], stack=stage_a) for n in ("qqT", "qkT", "lqT", "lkT"))
        gateT = sb("gateT", [P, EH, S], stack=stage_a)
        vpre = sb("vpre", [P, T, INNER], stack=stage_a)
        vact = sb("vact", [P, T, INNER], stack=stage_a)
        lk = sb("lk", [P, T, P], stack=stage_a)
        relu_m = sb("relu_m", [P, S], stack=stage_a)
        relu_sq = sb("relu_sq", [P, S], stack=stage_a)
        lin_m = sb("lin_m", [P, S], stack=stage_a)
        attnT = sb("attnT", [P, S], stack=stage_a)
        state = sb("state", [P, T, INNER], stack=stage_a)
        gatedT = sb("gatedT", [P, EH, S], stack=stage_a)
        KV_BANK = [2, 2, 3, 3, 4, 4, 5]

        def cols(i, n=P):
            return slice(i * n, (i + 1) * n)

        def a_tensor(pe, r):
            pe.wait_ge(a_gated, 4 * r)
            ln_tensor(pe, r)
            pe.wait_ge(a_res, 2 * r)
            for h in range(2):
                pe.wait_ge(ln_xT, 2 * r + h + 1)
                nc.tensor.matmul(bank[:, 2 + h, :], win_sb[:], xT[:, cols(h, HALF)], start=True, stop=True).then_inc(a_xproj, 1)
            for e in range(EH):
                for h in range(2):
                    nc.tensor.matmul(bank[:, 4 + 2 * e + h, :], wg_sb[:, cols(e)], xT[:, cols(h, HALF)],
                                     start=True, stop=True).then_inc(a_gproj, 1)
            for t in range(T):
                if t == 4:
                    pe.wait_ge(a_xs, 2 * r + 2)
                nc.tensor.matmul(bank[:, t // 2, cols(t % 2, INNER)], xT[:, cols(t)], wv_sb[:],
                                 start=True, stop=True).then_inc(a_vproj, 1)
            pe.wait_ge(a_gs, 4 * r + 2)
            pe.wait_ge(a_feat, 4 * r + 1)
            for t in range(T):
                nc.tensor.transpose(bank[:, 4 + t // 4, cols(t % 4)], lkT[:, cols(t)], ident[:]).then_inc(a_lktr, 1)
            pe.wait_ge(a_gs, 4 * r + 4)
            pe.wait_ge(a_feat, 4 * r + 3)
            for t in range(T):
                nc.tensor.matmul(bank[:, 6 + t // 4, cols(t % 4)], qkT[:, cols(t)], qqT[:, cols(t)],
                                 start=True, stop=True).then_inc(a_sq, 1)
            pe.wait_ge(a_feat, 4 * r + 4)
            pe.wait_ge(a_vbias, 4 * r + 2)
            for t in range(T):
                nc.tensor.matmul(bank[:, t // 4, cols(t % 4)], lkT[:, cols(t)], lqT[:, cols(t)],
                                 start=True, stop=True).then_inc(a_sl, 1)
            pe.wait_ge(a_v, 4 * r + 4)
            pe.wait_ge(a_lkt, 2 * r + 2)
            for t in range(T - 1):
                nc.tensor.matmul(bank[:, KV_BANK[t], cols(t % 2, INNER)], lk[:, t, :], vact[:, t, :],
                                 start=True, stop=True).then_inc(a_kv, 1)
            pe.wait_ge(a_at, 2 * r + 2)
            for e in range(EH):
                for t in range(T):
                    o = bank[:, (6 if e == 0 else 0) + t // 4, cols(t % 4)]
                    ins = nc.tensor.matmul(o, vact[:, t, cols(e)], attnT[:, cols(t)], start=True, stop=(t == 0))
                    if t > 0:
                        if e == 0:
                            pe.wait_ge(a_state, 7 * r + t)
                        ins = nc.tensor.matmul(o, state[:, t, cols(e)], lqT[:, cols(t)], start=False, stop=True)
                    ins.then_inc(a_o, 1)
            pe.wait_ge(a_gated, 4 * r + 4)
            for t in range(T):
                for e in range(EH):
                    ins = nc.tensor.matmul(bank[:, 2 + t // 4, cols(t % 4)], gatedT[:, e, cols(t)], wout_sb[:, e, :],
                                           start=(e == 0), stop=(e == EH - 1))
                ins.then_inc(a_out, 1)

        def a_scalar(a, r):
            ln_scalar(a, r)
            for h in range(2):
                a.wait_ge(a_xproj, 2 * r + h + 1)
                nc.scalar.activation(base[:, cols(h, HALF)], bank[:, 2 + h, :], ACT.Silu, bias=ca[:, 2:3]).then_inc(a_xs, 1)
            for e in range(EH):
                for h in range(2):
                    a.wait_ge(a_gproj, 4 * r + 2 * e + h + 1)
                    nc.scalar.activation(gateT[:, e, cols(h, HALF)], bank[:, 4 + 2 * e + h, :], ACT.Silu,
                                         bias=ca[:, e:e + 1]).then_inc(a_gs, 1)
            for k in range(4):
                a.wait_ge(a_vbias, 4 * r + k + 1)
                nc.scalar.activation(vact[:, 2 * k:2 * k + 2, :], vpre[:, 2 * k:2 * k + 2, :], ACT.Silu).then_inc(a_v, 1)
            for h in range(2):
                a.wait_ge(a_lktr, T * r + 4 * (h + 1))
                nc.scalar.activation(lk[:, 4 * h:4 * h + 4, :], bank[:, 4 + h, :].rearrange("p (t c) -> p t c", c=P),
                                     ACT.Copy).then_inc(a_lkt, 1)
            for h in range(2):
                a.wait_ge(a_u, 2 * r + h + 1)
                nc.scalar.activation(relu_sq[:, cols(h, HALF)], relu_m[:, cols(h, HALF)], ACT.Square).then_inc(a_usq, 1)

        def a_vector(v, step, r, b):
            ln_vector(v, step, r, b)
            v.wait_ge(a_xs, 2 * r + 2)
            for dst, c in ((lkT, 9), (qkT, 5), (qqT, 3), (lqT, 7)):
                nc.vector.tensor_scalar(dst[:], base[:], ca[:, c:c + 1], ca[:, c + 1:c + 2], ALU.mult, ALU.add).then_inc(a_feat, 1)
            for k in range(4):
                v.wait_ge(a_vproj, T * r + 2 * (k + 1))
                nc.vector.tensor_tensor(vpre[:, 2 * k:2 * k + 2, :], bank[:, k, :].rearrange("p (t c) -> p t c", c=INNER),
                                        bv_sb[:].unsqueeze(1).to_broadcast([P, 2, INNER]), ALU.add).then_inc(a_vbias, 1)
            for h in range(2):
                v.wait_ge(a_sq, T * r + 4 * (h + 1))
                nc.vector.scalar_tensor_tensor(
                    out=relu_m[:, cols(h, HALF)].rearrange("p (t c) -> p t c", c=P),
                    in0=bank[:, 6 + h, :].rearrange("p (t c) -> p t c", c=P), scalar=0.0,
                    in1=m_quad[:].unsqueeze(1).to_broadcast([P, 4, P]), op0=ALU.max, op1=ALU.mult).then_inc(a_u, 1)
            for h in range(2):
                v.wait_ge(a_sl, T * r + 4 * (h + 1))
                step.done(nc.vector.tensor_tensor(
                    lin_m[:, cols(h, HALF)].rearrange("p (t c) -> p t c", c=P),
                    bank[:, h, :].rearrange("p (t c) -> p t c", c=P),
                    m_lin[:].unsqueeze(1).to_broadcast([P, 4, P]), ALU.mult))
            step.wait()
            for h in range(2):
                v.wait_ge(a_usq, 2 * r + h + 1)
                nc.vector.tensor_tensor(attnT[:, cols(h, HALF)], relu_sq[:, cols(h, HALF)], lin_m[:, cols(h, HALF)],
                                        ALU.add).then_inc(a_at, 1)
            for t in range(1, T):
                v.wait_ge(a_kv, 7 * r + min(t + t % 2, T - 1))
                kv = bank[:, KV_BANK[t - 1], cols((t - 1) % 2, INNER)]
                if t == 1:
                    nc.vector.tensor_copy(state[:, t, :], kv).then_inc(a_state, 1)
                else:
                    v.wait_ge(a_state, 7 * r + t - 1)
                    nc.vector.tensor_tensor(state[:, t, :], kv, state[:, t - 1, :], ALU.add).then_inc(a_state, 1)
            for e in range(EH):
                for h in range(2):
                    v.wait_ge(a_o, 2 * T * r + T * e + 4 * (h + 1))
                    nc.vector.tensor_tensor(gatedT[:, e, cols(h, HALF)], bank[:, (6 if e == 0 else 0) + h, :],
                                            gateT[:, e, cols(h, HALF)], ALU.mult).then_inc(a_gated, 1)
            v.wait_ge(biased, r)
            for h in range(2):
                v.wait_ge(a_out, T * r + 4 * (h + 1))
                xr = xres[:, bass.ds(b * T + 4 * h, 4), :]
                nc.vector.tensor_tensor(xr, bank[:, 2 + h, :].rearrange("p (t c) -> p t c", c=P), xr, ALU.add).then_inc(a_res, 1)
            v.wait_ge(a_res, 2 * r + 2)
        stage_a.close()

        stage_f = ExitStack()
        def small(name, dt=F32):
            return sb(name, [P, T, E], dt, stack=stage_f)
        lg, ex, pr, eq, key, pr2, tmp = (small(n) for n in ("lg", "ex", "pr", "eq", "key", "pr2", "tmp"))
        oh = [small("oh1"), small("oh2")]
        chosen = small("chosen", BF16)
        rowmat, keepmat = small("rowmat"), small("keepmat")
        nmax, rsum, rinv, rk = (sb(n, [P, T], stack=stage_f) for n in ("nmax", "rsum", "rinv", "rk"))
        ptop = sb("ptop", [P, 2, T], stack=stage_f)
        kept = sb("kept", [P, 2, T], stack=stage_f)
        wtok = sb("wtok", [P, 2, T], stack=stage_f)
        rowf = sb("rowf", [P, 2, T], stack=stage_f)
        skip = sb("skip", [P, 2, T], stack=stage_f)
        row_g = sb("row_g", [P, 2, T], U32, stack=stage_f)
        row_s = sb("row_s", [P, 2, T], U32, stack=stage_f)
        xs_sb = sb("xs_sb", [P, ST, P], stack=stage_f)
        xsT = sb("xsT", [P, SLOTS], stack=stage_f)
        hT = sb("hT", [P, 2, HC, CAP], stack=stage_f)
        yT = sb("yT", [P, SLOTS], stack=stage_f)
        ys = sb("ys", [P, ST, P], stack=stage_f)
        yg = sb("yg", [P, 2, T, P], stack=stage_f)
        TR = [(0, 0, 4), (1, 4, 8), (2, 8, ST)]

        def over_e(t):
            return t.unsqueeze(2).to_broadcast([P, T, E])

        def f_tensor(pe, m, n):
            pe.wait_ge(f_ha, E * m)
            pe.wait_ge(f_ya, E * m)
            ln_tensor(pe, n)
            for t in range(T):
                if t % 4 == 0:
                    pe.wait_ge(ln_xT, 2 * n + t // 4 + 1)
                ins = nc.tensor.matmul(bank[:, 2, t * E:(t + 1) * E], xT[:, cols(t)], wr_sb[:], start=True, stop=True)
            ins.then_inc(f_lg, 1)
            pe.wait_ge(f_m, m + 1)
            pos = bank[:, 3, 0:T * E].rearrange("p (t e) -> p t e", e=E)
            nc.tensor.matmul(bank[:, 3, 0:T * E], before[:], chosen[:].rearrange("p t e -> p (t e)"), start=True, stop=False)
            for t in range(T - 1):
                ins = nc.tensor.matmul(pos[:, t + 1:T, :], ones[:], chosen[:, t:t + 1, :].to_broadcast([P, T - 1 - t, E]),
                                       start=False, stop=(t == T - 2))
            ins.then_inc(f_pos, 1)
            pe.wait_ge(f_ld, 16 * (m + 1))
            for bk, lo, hi in TR:
                for i in range(lo, hi):
                    nc.tensor.transpose(bank[:, bk, cols(i - lo)], xs_sb[:, i, :], ident[:]).then_inc(f_str, 1)
            pe.wait_ge(f_xs, 3 * (m + 1))

            def up(e):
                if e >= 2:
                    pe.wait_ge(f_ha, E * m + e - 1)
                    pe.wait_ge(f_hd, E * m + e - 1)
                for c in range(HC):
                    ins = nc.tensor.matmul(bank[:, 2 + 2 * (e % 2) + c // 2, cols(c % 2, CAP)], w1_sb[:, e, cols(c)],
                                           xsT[:, cols(e, CAP)], start=True, stop=True)
                    if c % 2:
                        ins.then_inc(f_h, 1)

            def down(e):
                pe.wait_ge(f_ha, E * m + e + 1)
                pe.wait_ge(f_hd, E * m + e + 1)
                if e >= 2:
                    pe.wait_ge(f_ya, E * m + e - 1)
                for c in range(HC):
                    ins = nc.tensor.matmul(bank[:, 6 + e % 2, 0:CAP], w2_sb[:, e, c, :], hT[:, e % 2, c, :],
                                           start=(c == 0), stop=(c == HC - 1))
                ins.then_inc(f_y, 1)

            up(0)
            for e in range(1, E):
                up(e)
                down(e - 1)
            down(E - 1)
            pe.wait_ge(f_ya, E * (m + 1))
            for bk, lo, hi in TR:
                for i in range(lo, hi):
                    nc.tensor.transpose(bank[:, bk, cols(i - lo)], yT[:, cols(i)], ident[:]).then_inc(f_ytr, 1)

        def f_scalar(a, m, n):
            ln_scalar(a, n)
            a.wait_ge(f_sub, m + 1)
            nc.scalar.activation(ex[:], lg[:], ACT.Exp).then_inc(f_exp, 1)
            for bk, lo, hi in TR:
                a.wait_ge(f_str, ST * m + hi)
                nc.scalar.activation(xsT[:, lo * P:hi * P], bank[:, bk, 0:(hi - lo) * P], ACT.Copy).then_inc(f_xs, 1)

            def hidden(e):
                a.wait_ge(f_h, 2 * E * m + 2 * e + 1)
                if e >= 2:
                    a.wait_ge(f_y, E * m + e - 1)
                for c in range(2):
                    ins = nc.scalar.activation(hT[:, e % 2, c, :], bank[:, 2 + 2 * (e % 2), cols(c, CAP)], ACT.Relu,
                                               bias=b1_sb[:, e * HC + c:e * HC + c + 1])
                ins.then_inc(f_ha, 1)

            def answer(e):
                a.wait_ge(f_y, E * m + e + 1)
                nc.scalar.activation(yT[:, cols(e, CAP)], bank[:, 6 + e % 2, 0:CAP], ACT.Identity,
                                     bias=b2_sb[:, e:e + 1]).then_inc(f_ya, 1)

            hidden(0)
            for e in range(1, E):
                hidden(e)
                answer(e - 1)
            answer(E - 1)

        def f_vector(v, step, m, n, b):
            v.wait_ge(f_ld, 16 * m)
            ln_vector(v, step, n, b)
            v.wait_ge(f_lg, m + 1)
            logits = bank[:, 2, 0:T * E].rearrange("p (t e) -> p t e", e=E)
            step.then(nc.vector.tensor_reduce(nmax[:], logits, X_AXIS, ALU.max))
            nc.vector.tensor_tensor(lg[:], logits, over_e(nmax[:]), ALU.subtract).then_inc(f_sub, 1)
            v.wait_ge(f_exp, m + 1)
            step.then(nc.vector.tensor_reduce(rsum[:], ex[:], X_AXIS, ALU.add))
            step.then(nc.vector.reciprocal(rinv[:], rsum[:]))
            step.then(nc.vector.tensor_tensor(pr[:], ex[:], over_e(rinv[:]), ALU.mult))
            p_now = pr
            for k in range(2):
                step.then(nc.vector.tensor_reduce(ptop[:, k, :], p_now[:], X_AXIS, ALU.max))
                step.then(nc.vector.tensor_tensor(eq[:], p_now[:], over_e(ptop[:, k, :]), ALU.is_equal))
                step.then(nc.vector.tensor_tensor(key[:], eq[:], rev[:].unsqueeze(1).to_broadcast([P, T, E]), ALU.mult))
                step.then(nc.vector.tensor_reduce(rk[:], key[:], X_AXIS, ALU.max))
                step.then(nc.vector.tensor_tensor(oh[k][:], key[:], over_e(rk[:]), ALU.is_equal))
                if k == 0:
                    step.then(nc.vector.scalar_tensor_tensor(out=pr2[:], in0=oh[0][:], scalar=-2.0, in1=pr[:],
                                                             op0=ALU.mult, op1=ALU.add))
                    p_now = pr2
            nc.vector.tensor_tensor(chosen[:], oh[0][:], oh[1][:], ALU.add).then_inc(f_m, 1)
            v.wait_ge(f_pos, m + 1)
            pos = bank[:, 3, 0:T * E].rearrange("p (t e) -> p t e", e=E)
            step.done(nc.vector.tensor_scalar(keepmat[:], pos, float(CAP), None, ALU.is_lt))
            step.then(nc.vector.tensor_scalar(tmp[:], pos, float(CAP - 1), None, ALU.min))
            step.then(nc.vector.tensor_tensor(rowmat[:], tmp[:],
                                              rowbase[:, bass.ds(b, 1), :].to_broadcast([P, T, E]), ALU.add))
            for k in range(2):
                step.then(nc.vector.tensor_tensor(tmp[:], oh[k][:], rowmat[:], ALU.mult))
                step.then(nc.vector.tensor_reduce(rowf[:, k, :], tmp[:], X_AXIS, ALU.add))
                step.then(nc.vector.tensor_tensor(tmp[:], oh[k][:], keepmat[:], ALU.mult))
                step.then(nc.vector.tensor_reduce(kept[:, k, :], tmp[:], X_AXIS, ALU.add))
            step.done(nc.vector.tensor_copy(row_g[:], rowf[:]))
            step.then(nc.vector.tensor_scalar(skip[:], kept[:], -SKIPPED, SKIPPED, ALU.mult, ALU.add))
            step.done(nc.vector.tensor_tensor(wtok[:], ptop[:], kept[:], ALU.mult))
            nc.vector.tensor_tensor(row_s[:], rowf[:], skip[:], ALU.add).then_inc(f_idx, 1)
            for e in range(E):
                v.wait_ge(f_h, 2 * E * m + 2 * e + 2)
                if e >= 2:
                    v.wait_ge(f_y, E * m + e - 1)
                for c in range(2, HC):
                    ins = nc.vector.tensor_scalar(hT[:, e % 2, c, :], bank[:, 3 + 2 * (e % 2), cols(c % 2, CAP)],
                                                  b1_sb[:, e * HC + c:e * HC + c + 1], 0.0, ALU.add, ALU.max)
                ins.then_inc(f_hd, 1)
            v.wait_ge(f_st, 16 * m)
            for bk, lo, hi in TR:
                v.wait_ge(f_ytr, ST * m + hi)
                nc.vector.tensor_copy(ys[:, lo:hi, :], bank[:, bk, 0:(hi - lo) * P].rearrange("p (t c) -> p t c", c=P))\
                    .then_inc(f_ys, 1)
            v.wait_ge(f_ga, 256 * m)
            for k in range(2):
                for t in range(T):
                    xr = xres[:, bass.ds(b * T + t, 1), :].rearrange("p a c -> p (a c)")
                    ins = nc.vector.scalar_tensor_tensor(out=xr, in0=yg[:, k, t, :], scalar=wtok[:, k, t:t + 1], in1=xr,
                                                         op0=ALU.mult, op1=ALU.add)
                    ins.then_inc(f_comb, 1)
                v.wait_ge(f_comb, 2 * T * m + T * (k + 1))

        def f_pool(p, step, m, n, b):
            ln_pool(p, step, n, b)
            hold(p, f_idx, m + 1)
            p.wait_ge(zeroed, 16)
            for k in range(2):
                for t in range(T):
                    nc.gpsimd.indirect_dma_start(out=xslots[:, :], out_offset=bass.IndirectOffsetOnAxis(ap=row_s[:, k, t:t + 1], axis=0),
                                                 in_=xhat[:, t, :], in_offset=None,
                                                 bounds_check=B * SLOTS - 1, oob_is_err=False).then_inc(f_sc, 16)
            p.wait_ge(f_st, 16 * (m + 1))
            hold(p, f_comb, 2 * T * m)
            for k in range(2):
                for t in range(T):
                    nc.gpsimd.indirect_dma_start(out=yg[:, k, t, :], out_offset=None, in_=yslots[:, :],
                                                 in_offset=bass.IndirectOffsetOnAxis(ap=row_g[:, k, t:t + 1], axis=0),
                                                 bounds_check=B * SLOTS - 1, oob_is_err=False).then_inc(f_ga, 16)

        def f_sync(sp, m, b):
            sp.wait_ge(f_sc, 256 * m)
            sp.dma_start(xs_sb[:], xslots[bass.ds(b * SLOTS, SLOTS), :].rearrange("(i p) c -> p i c", p=P)).then_inc(f_ld, 16)
            sp.wait_ge(f_ys, 3 * (m + 1))
            sp.dma_start(yslots[bass.ds(b * SLOTS, SLOTS), :].rearrange("(i p) c -> p i c", p=P), ys[:]).then_inc(f_st, 16)
        stage_f.close()

        stage_c = ExitStack()
        wall = sb("wall", [P, PAIRS, WCOLS], stack=stage_c)
        wl_sb = sb("wl_sb", [P, PAIRS, P], stack=stage_c)
        ws = [sb(f"ws{i}", [P, WCOLS], stack=stage_c) for i in range(2)]
        qst = [[sb(f"q{i}{h}", [P, 2, S], F32R, stack=stage_c) for h in range(2)] for i in range(2)]
        kst = [[sb(f"k{i}{h}", [P, S], F32R, stack=stage_c) for h in range(2)] for i in range(2)]
        vst = [sb(f"v{i}", [P, T, P], stack=stage_c) for i in range(2)]
        prob = [[sb(f"prob{i}{h}", [P, S], stack=stage_c) for h in range(2)] for i in range(2)]
        vsc = [sb(f"vsc{i}", [P, P], stack=stage_c) for i in range(2)]
        nmx = sb("nmx", [P, 4], stack=stage_c)
        zsum = sb("zsum", [P, 4], stack=stage_c)
        zinv = sb("zinv", [P, 4], stack=stage_c)
        ctxT = sb("ctxT", [P, PAIRS, S], stack=stage_c)
        SC = [(0, 1), (2, 3)]
        CX = (4, 5)
        PJ = (6, 7)
        SPAN = 2 * T
        LEAD = 2

        def rows(h):
            return slice(h * HD, (h + 1) * HD)

        def project(pe, par, pr_i, units):
            w = ws[par]
            for k in units:
                if k == 0:
                    pe.wait_ge(c_stage, pr_i + 1)
                    pe.wait_ge(c_pev, 6 * pr_i)
                elif k >= 2:
                    pe.wait_ge(c_pev, 6 * pr_i + k - 1)
                if k < 4:
                    ins = nc.tensor.matmul(bank[:, PJ[k % 2], :], w[:, (WQ if k < 2 else WK):(WQ if k < 2 else WK) + P],
                                           xT[:, cols(k % 2, HALF)], start=True, stop=True)
                else:
                    for t in range(4):
                        ins = nc.tensor.matmul(bank[:, PJ[k % 2], cols(t)], xT[:, cols(4 * (k - 4) + t)], w[:, WV:WV + P],
                                               start=True, stop=True)
                ins.then_inc(c_proj, 1)

        def proj_hi(a, par, pr_i, k):
            w = ws[par]
            a.wait_ge(c_proj, 6 * pr_i + k + 1)
            for h in range(2):
                r = rows(h)
                dst = qst[par][h][r, 0, cols(k % 2, HALF)] if k < 2 else kst[par][h][r, cols(k % 2, HALF)]
                bias = w[r, BQ:BQ + 1] if k < 2 else w[r, BK:BK + 1]
                nc.scalar.activation(dst, bank[r, PJ[k % 2], :], ACT.Identity, bias=bias).then_inc(c_hi, 1)

        def proj_lo(v, par, pr_i, k):
            w = ws[par]
            if k >= 4:
                v.wait_ge(c_proj, 6 * pr_i + k + 1)
                nc.vector.tensor_tensor(vst[par][:, 4 * (k - 4):4 * (k - 3), :],
                                        bank[:, PJ[k % 2], :].rearrange("p (t c) -> p t c", c=P),
                                        w[:, BV:BV + P].unsqueeze(1).to_broadcast([P, 4, P]), ALU.add).then_inc(c_pev, 1)
                return
            for h in range(2):
                r, o = rows(h), rows(1 - h)
                v.wait_ge(c_hi, 8 * pr_i + 2 * k + h + 1)
                if k < 2:
                    hi, lo = qst[par][h][r, 0, cols(k, HALF)], qst[par][h][r, 1, cols(k, HALF)]
                    bias = w[r, BQ:BQ + 1]
                else:
                    hi, lo = kst[par][h][r, cols(k - 2, HALF)], kst[par][h][o, cols(k - 2, HALF)]
                    bias = w[r, BK:BK + 1]
                ins = nc.vector.scalar_tensor_tensor(out=lo, in0=bank[r, PJ[k % 2], :], scalar=bias, in1=hi.bitcast(F32),
                                                     op0=ALU.add, op1=ALU.subtract)
            ins.then_inc(c_pev, 1)

        def q_copy(sp, par, pr_i):
            sp.wait_ge(c_pev, 6 * pr_i + 2)
            for h in range(2):
                src = qst[par][h][rows(h), :, :].bitcast(F32)
                dst = qst[par][h][rows(1 - h), :, :].bitcast(F32)
                sp.dma_start(dst, src).then_inc(c_dup, 16)

        def scores(pe, par, j, g, first=False):
            for h in range(2):
                if not first:
                    pe.wait_ge(c_exp, 2 * g + h - 1)
                for n in range(2):
                    o = bank[:, SC[h][n], :]
                    kk = kst[par][h][:, cols(j)]
                    nc.tensor.matmul(o, kk, qst[par][h][:, 0, cols(n, HALF)], start=True, stop=False)
                    ins = nc.tensor.matmul(o, kk, qst[par][h][:, 1, cols(n, HALF)], start=False, stop=True)
                ins.then_inc(c_qk, 1)

        def context(pe, j, g, pr_i):
            s = j % 2
            if j == 0:
                pe.wait_ge(c_ctx, 2 * pr_i)
            pe.wait_ge(c_vs, g + 1)
            for n in range(2):
                for h in range(2):
                    ins = nc.tensor.matmul(bank[rows(h), CX[n], :], vsc[s][:, rows(h)], prob[s][h][:, cols(n, HALF)],
                                           start=(j == 0), stop=(j == T - 1))
            ins.then_inc(c_av, 1)

        def score_max(v, g, s):
            for h in range(2):
                v.wait_ge(c_qk, 2 * g + h + 1)
                nc.vector.tensor_reduce(nmx[:, 2 * s + h:2 * s + h + 1], bank[:, SC[h][0]:SC[h][0] + 2, :],
                                        mybir.AxisListType.XY, ALU.max, negate=True).then_inc(c_max, 1)

        def score_exp(a, g, s):
            for h in range(2):
                a.wait_ge(c_max, 2 * g + h + 1)
                nc.scalar.activation(prob[s][h][:].rearrange("p (n c) -> p n c", c=HALF), bank[:, SC[h][0]:SC[h][0] + 2, :],
                                     ACT.Exp, bias=nmx[:, 2 * s + h:2 * s + h + 1],
                                     accum_out=zsum[:, 2 * s + h:2 * s + h + 1]).then_inc(c_exp, 1)

        def scale_v(v, step, par, j, g):
            s = j % 2
            v.wait_ge(c_exp, 2 * g + 2)
            step.then(nc.vector.reciprocal(zinv[:, 2 * s:2 * s + 2], zsum[:, 2 * s:2 * s + 2]))
            nc.vector.tensor_tensor(vsc[s][:].rearrange("p (h c) -> p h c", c=HD),
                                    vst[par][:, j, :].rearrange("p (h c) -> p h c", c=HD),
                                    zinv[:, 2 * s:2 * s + 2].unsqueeze(2).to_broadcast([P, 2, HD]), ALU.mult).then_inc(c_vs, 1)

        UNITS = {0: (0, 1), 2: (2, 3), 4: (4, 5)}

        def steps_of(g0, pair0, last):
            for s in range(SPAN):
                yield s, s // T, s % T, g0 + s, pair0 + s // T

        def c_body_tensor(pe, g0, pair0, last):
            for s, par, j, g, pi in steps_of(g0, pair0, last):
                if j in UNITS and not (last and par == 1):
                    project(pe, 1 - par, pi + 1, UNITS[j])
                context(pe, j, g, pi)
                if not (last and s + LEAD >= SPAN):
                    j2, par2 = (j + LEAD) % T, (par + (j + LEAD) // T) % 2
                    if j2 == 0:
                        pe.wait_ge(c_dup, 32 * (pi + 2))
                        pe.wait_ge(c_pev, 6 * (pi + 1) + 4)
                    scores(pe, par2, j2, g + LEAD)

        def c_body_scalar(a, g0, pair0, pair_row, last):
            for s, par, j, g, pi in steps_of(g0, pair0, last):
                if j in (0, 2) and not (last and par == 1):
                    for k in UNITS[j]:
                        proj_hi(a, 1 - par, pi + 1, k)
                if not (last and s + LEAD >= SPAN):
                    score_exp(a, g + LEAD, s % 2)
                if j == T - 1:
                    a.wait_ge(c_av, g + 1)
                    for n in range(2):
                        nc.scalar.activation(ctxT[:, bass.ds(pair_row + par, 1), cols(n, HALF)].rearrange("p a c -> p (a c)"),
                                             bank[:, CX[n], :], ACT.Copy).then_inc(c_ctx, 1)

        def c_body_vector(v, step, g0, pair0, last):
            for s, par, j, g, pi in steps_of(g0, pair0, last):
                if j in UNITS and not (last and par == 1):
                    for k in UNITS[j]:
                        proj_lo(v, 1 - par, pi + 1, k)
                if not (last and s + 1 >= SPAN):
                    if last and s + LEAD >= SPAN:
                        v.wait_ge(c_av, g)
                    scale_v(v, step, (par + (j + 1) // T) % 2, (j + 1) % T, g + 1)
                if not (last and s + LEAD >= SPAN):
                    score_max(v, g + LEAD, s % 2)

        def c_stage_pair(p, pr_i, pair_row, par, first):
            if not first:
                hold(p, c_pev, 6 * (pr_i - 1))
            nc.gpsimd.tensor_copy(ws[par][:], wall[:, bass.ds(pair_row, 1), :].rearrange("p a c -> p (a c)")).then_inc(c_stage, 1)

        def c_tensor(pe, r, n):
            ln_tensor(pe, n)
            pe.wait_ge(ln_xT, 2 * n + 2)
            project(pe, 0, PAIRS * r, range(6))
            pe.wait_ge(c_dup, 32 * (PAIRS * r + 1))
            pe.wait_ge(c_pev, 6 * PAIRS * r + 4)
            scores(pe, 0, 0, PAIRS * T * r, first=True)
            scores(pe, 0, 1, PAIRS * T * r + 1)
            with pe.Fori(0, PAIRS // 2 - 1) as it:
                c_body_tensor(pe, PAIRS * T * r + SPAN * it, PAIRS * r + 2 * it, False)
            it = PAIRS // 2 - 1
            c_body_tensor(pe, PAIRS * T * r + SPAN * it, PAIRS * r + 2 * it, True)
            pe.wait_ge(c_ctx, 2 * PAIRS * (r + 1))
            for t in range(T):
                for q in range(PAIRS):
                    ins = nc.tensor.matmul(bank[:, PJ[t // 4], cols(t % 4)], ctxT[:, q, cols(t)], wl_sb[:, q, :],
                                           start=(q == 0), stop=(q == PAIRS - 1))
                ins.then_inc(c_out, 1)

        def c_scalar(a, r, n):
            ln_scalar(a, n)
            for k in range(4):
                proj_hi(a, 0, PAIRS * r, k)
            for j in range(2):
                score_exp(a, PAIRS * T * r + j, j)
            with a.Fori(0, PAIRS // 2 - 1) as it:
                c_body_scalar(a, PAIRS * T * r + SPAN * it, PAIRS * r + 2 * it, 2 * it, False)
            it = PAIRS // 2 - 1
            c_body_scalar(a, PAIRS * T * r + SPAN * it, PAIRS * r + 2 * it, 2 * it, True)

        stage_c.close()

        block = keep.enter_context(nc.Block())

        @block.sync
        def _(sp):
            sp.dma_start(xres[:], x.rearrange("(t p) c -> p t c", p=P)).then_inc(load_sem, 16)
            for dst, src in ((wv_sb, wv), (wg_sb, wg), (win_sb, win), (ca, cols_a)):
                sp.dma_start(dst[:], src).then_inc(load_sem, 16)
            sp.dma_start(wout_sb[:], wout.rearrange("(e p) c -> p e c", p=P)).then_inc(load_sem, 16)
            sp.dma_start(bv_sb[:], bv.partition_broadcast(P)).then_inc(load_sem, 16)
            sp.dma_start(bout_sb[:], bout.partition_broadcast(P)).then_inc(load_sem, 16)
            sp.dma_start(bl_sb[:], bl.partition_broadcast(P)).then_inc(load_sem, 16)
            sp.dma_start(wr_sb[:], wr).then_inc(load_sem, 16)
            sp.dma_start(w1_sb[:], w1.rearrange("e p h -> p e h")).then_inc(load_sem, 16)
            sp.dma_start(w2_sb[:], w2.rearrange("e (c p) n -> p e c n", p=P)).then_inc(load_sem, 16)
            sp.dma_start(b1_sb[:], b1).then_inc(load_sem, 16)
            sp.dma_start(b2_sb[:], b2).then_inc(load_sem, 16)
            with sp.Fori(0, B) as b:
                f_sync(sp, b + 1, b)
            sp.wait_ge(f_comb, 2 * T * (B + 1))
            sp.dma_start(wall[:, :, 0:3 * P], wqkv.rearrange("p a c -> p a c")).then_inc(load_c, 16)
            sp.dma_start(wall[:, :, BQ:BQ + 2], bqk).then_inc(load_c, 16)
            sp.dma_start(wall[:, :, BV:BV + P], bvv.partition_broadcast(P)).then_inc(load_c, 16)
            sp.dma_start(wl_sb[:], wl).then_inc(load_c, 16)
            with sp.Fori(0, B) as b:
                pair = PAIRS * (b + 1)
                q_copy(sp, 0, pair)
                with sp.Fori(0, PAIRS // 2 - 1) as it:
                    q_copy(sp, 1, pair + 2 * it + 1)
                    q_copy(sp, 0, pair + 2 * it + 2)
                q_copy(sp, 1, pair + PAIRS - 1)
            with sp.Fori(0, B) as b:
                f_sync(sp, B + b + 1, b)
                sp.wait_ge(f_comb, 2 * T * (B + b + 2))
                sp.dma_start(out[bass.ds(b * S, S), :].rearrange("(t p) c -> p t c", p=P),
                             xres[:, bass.ds(b * T, T), :]).then_inc(stored, 16)
            sp.wait_ge(stored, 16 * B)

        @block.gpsimd
        def _(p):
            step = Steps(p, pool_step)
            step.done(nc.gpsimd.memset(minus_half[:], -0.5))
            step.done(nc.gpsimd.memset(ident[:], 1.0))
            step.done(nc.gpsimd.memset(before[:], 1.0))
            step.done(nc.gpsimd.memset(ones[:], 1.0))
            step.done(nc.gpsimd.memset(m_quad[:], 0.0))
            step.done(nc.gpsimd.memset(m_lin[:], 0.0))
            step.done(nc.gpsimd.iota(rev[:], [[-1, E]], base=E, channel_multiplier=0, allow_small_or_imprecise_dtypes=True))
            step.done(nc.gpsimd.iota(rowbase[:], [[SLOTS, B], [CAP, E]], base=0, channel_multiplier=0,
                                     allow_small_or_imprecise_dtypes=True))
            step.done(nc.gpsimd.memset(xhat[:], 0.0))
            step.wait()
            step.then(nc.gpsimd.affine_select(out=ident[:], in_=ident[:], compare_op=ALU.is_equal, fill=0.0, base=0,
                                              pattern=[[-1, P]], channel_multiplier=1))
            step.then(nc.gpsimd.affine_select(out=before[:], in_=before[:], compare_op=ALU.is_gt, fill=0.0, base=0,
                                              pattern=[[1, P]], channel_multiplier=-1))
            for g in range(P // GROUP):
                r = slice(g * GROUP, (g + 1) * GROUP)
                step.then(nc.gpsimd.memset(m_quad[r, r], float(INNER) ** -0.5))
                if g < P // GROUP - 1:
                    step.then(nc.gpsimd.memset(m_lin[r, (g + 1) * GROUP:P], 1.0))
            for g in range(P // GROUP):
                r = slice(g * GROUP, (g + 1) * GROUP)
                step.then(nc.gpsimd.affine_select(out=m_quad[r, r], in_=m_quad[r, r], compare_op=ALU.is_ge, fill=0.0, base=0,
                                                  pattern=[[1, GROUP]], channel_multiplier=-1))
            for slots, i in [(d, i) for d in (xslots, yslots) for i in range(B * ST // T)]:
                nc.gpsimd.dma_start(slots[i * S:(i + 1) * S, :].rearrange("(t p) c -> p t c", p=P), xhat[:]).then_inc(zeroed, 16)
            p.wait_ge(zeroed, 32 * (B * ST // T))
            for s, count in per_row.items():
                p.sem_inc(s, count)
            p.sem_inc(consts, 1)
            p.wait_ge(load_sem, LOADS)

            def looped(body, count, per_body):
                start = step.n
                with p.Fori(0, count) as b:
                    step.n = start + b * per_body
                    body(b)
                step.n = start + count * per_body

            looped(lambda b: ln_pool(p, step, b + 1, b, bout_sb), B, 1)
            looped(lambda b: f_pool(p, step, b + 1, B + b + 1, b), B, 1)

            def c_pool(b):
                ln_pool(p, step, 2 * B + b + 1, b, bl_sb)
                pair = PAIRS * (b + 1)
                c_stage_pair(p, pair, 0, 0, True)
                with p.Fori(0, PAIRS // 2 - 1) as it:
                    c_stage_pair(p, pair + 2 * it + 1, 2 * it + 1, 1, False)
                    c_stage_pair(p, pair + 2 * it + 2, 2 * it + 2, 0, False)
                c_stage_pair(p, pair + PAIRS - 1, PAIRS - 1, 1, False)
            p.wait_ge(load_c, 64)
            step.done(nc.gpsimd.tensor_scalar(wall[:, :, WQ:WQ + P], wall[:, :, WQ:WQ + P], HD ** -0.5, None, ALU.mult))
            step.then(nc.gpsimd.tensor_scalar(wall[:, :, BQ:BQ + 1], wall[:, :, BQ:BQ + 1], HD ** -0.5, None, ALU.mult))
            looped(c_pool, B, 1)
            looped(lambda b: f_pool(p, step, B + b + 1, 3 * B + b + 1, b), B, 1)

        @block.scalar
        def _(a):
            a.wait_ge(consts, 1)
            a.wait_ge(load_sem, LOADS)
            with a.Fori(0, B) as b:
                a_scalar(a, b + 1)
            with a.Fori(0, B) as b:
                f_scalar(a, b + 1, B + b + 1)
            with a.Fori(0, B) as b:
                c_scalar(a, b + 1, 2 * B + b + 1)
            with a.Fori(0, B) as b:
                f_scalar(a, B + b + 1, 3 * B + b + 1)

        @block.vector
        def _(v):
            v.wait_ge(consts, 1)
            v.wait_ge(load_sem, LOADS)
            step = Steps(v, dve_step)

            def looped(body, count):
                start = step.n
                with v.Fori(0, count) as b:
                    step.n = start + b * per_body[body]
                    body(b)
                step.n = start + count * per_body[body]

            def row_a(b):
                a_vector(v, step, b + 1, b)

            def row_f(f):
                def body(b):
                    f_vector(v, step, f * B + b + 1, (1 + 2 * f) * B + b + 1, b)
                return body

            def row_c(b):
                n, r = 2 * B + b + 1, b + 1
                ln_vector(v, step, n, b)
                for k in range(6):
                    proj_lo(v, 0, PAIRS * r, k)
                g0 = PAIRS * T * r
                for j in range(2):
                    score_max(v, g0 + j, j)
                scale_v(v, step, 0, 0, g0)
                begin = step.n
                with v.Fori(0, PAIRS // 2 - 1) as it:
                    step.n = begin + SPAN * it
                    c_body_vector(v, step, g0 + SPAN * it, PAIRS * r + 2 * it, False)
                it = PAIRS // 2 - 1
                step.n = begin + SPAN * it
                c_body_vector(v, step, g0 + SPAN * it, PAIRS * r + 2 * it, True)
                v.wait_ge(biased, B + b + 1)
                for h in range(2):
                    v.wait_ge(c_out, T * r + 4 * (h + 1))
                    xr = xres[:, bass.ds(b * T + 4 * h, 4), :]
                    nc.vector.tensor_tensor(xr, bank[:, PJ[h], :].rearrange("p (t c) -> p t c", c=P), xr, ALU.add).then_inc(c_res, 1)
                v.wait_ge(c_res, 2 * r + 2)

            row_f1, row_f2 = row_f(0), row_f(1)
            STEPS_F = T + 4 + 5 + 1 + 5 + 3 + 8 + 3
            per_body = {row_a: T + 2, row_f1: STEPS_F, row_f2: STEPS_F, row_c: T + PAIRS * T}
            looped(row_a, B)
            looped(row_f1, B)
            looped(row_c, B)
            looped(row_f2, B)

        @block.tensor
        def _(pe):
            pe.wait_ge(consts, 1)
            pe.wait_ge(load_sem, LOADS)
            with pe.Fori(0, B) as b:
                a_tensor(pe, b + 1)
            with pe.Fori(0, B) as b:
                f_tensor(pe, b + 1, B + b + 1)
            with pe.Fori(0, B) as b:
                c_tensor(pe, b + 1, 2 * B + b + 1)
            with pe.Fori(0, B) as b:
                f_tensor(pe, B + b + 1, 3 * B + b + 1)


LOADS = 16 * 14


def kernel(**inputs):
    import numpy as np
    import concourse.bacc as bacc
    from concourse.bass_utils import run_bass_kernel_spmd

    def get(name):
        return np.asarray(inputs["L0_" + name])

    def attn(name):
        return get("attn_a_" + name)

    cols_a = np.stack([*attn("bg").reshape(EH, P), attn("bin_")] +
                      [attn(n) for n in ("g_qq", "b_qq", "g_qk", "b_qk", "g_lq", "b_lq", "g_lk", "b_lk")], axis=1)
    wqkv = np.stack([get(f"attn_b_{c}_w").reshape(PAIRS, P, P).transpose(2, 0, 1) for c in "qkv"], axis=2).reshape(P, PAIRS, 3 * P)
    bqk = np.stack([get(f"attn_b_{c}_b").reshape(PAIRS, P).T for c in "qk"], axis=2)
    arrays = {
        "x": attn("x").reshape(B * S, P), "wv": attn("Wv"), "bv": attn("bv"), "wg": attn("Wg"), "win": attn("Win"),
        "wout": attn("Wout"), "bout": attn("bout"), "cols_a": cols_a, "wr": get("ffn_Wr"), "w1": get("ffn_W1"),
        "b1": get("ffn_b1").reshape(E * HC, P).T, "w2": get("ffn_W2"), "b2": get("ffn_b2").T,
        "wqkv": wqkv, "bqk": bqk, "bvv": get("attn_b_v_b").reshape(PAIRS, P),
        "wl": get("attn_b_l_w").T.reshape(PAIRS, P, P).transpose(1, 0, 2), "bl": get("attn_b_l_b").reshape(P),
    }
    arrays = {n: np.ascontiguousarray(a) for n, a in arrays.items()}
    nc = bacc.Bacc("TRN2", target_bir_lowering=False, num_devices=1)
    args = {n: nc.dram_tensor("in_" + n, a.shape, mybir.dt.from_np(a.dtype), kind="ExternalInput").ap() for n, a in arrays.items()}
    result = nc.dram_tensor("out_x", (B * S, P), F32, kind="ExternalOutput").ap()
    bass_hybrid(nc, **args, out=result)
    r = run_bass_kernel_spmd(nc, [{"in_" + n: a for n, a in arrays.items()}], core_ids=[0])
    return r.results[0]["out_x"].reshape(B, S, P)
```

```python
from contextlib import ExitStack

import concourse.bass as bass
from concourse import mybir

F32 = mybir.dt.float32
F32R = mybir.dt.float32r
BF16 = mybir.dt.bfloat16
U32 = mybir.dt.uint32
I32 = mybir.dt.int32
ALU = mybir.AluOpType
ACT = mybir.ActivationFunctionType
X_AXIS = mybir.AxisListType.X

P = 128
B = 4
S = 1024
T = S // P
HALF = 512
GROUP = 32
INNER = 256
EH = INNER // P
E = 8
CAP = int(S / E * 1.25)
HID = 512
HC = HID // P
SLOTS = E * CAP
ST = SLOTS // P
HEADS = 16
HD = 64
PAIRS = HEADS // 2
EPS = 1e-5
SKIPPED = float(4 * B * SLOTS)
WQ, WK, WV, BQ, BK, BV, WCOLS = 0, P, 2 * P, 3 * P, 3 * P + 1, 3 * P + 2, 4 * P + 2


def bass_hybrid(nc, x, wv, bv, wg, win, wout, bout, cols_a, wr, w1, b1, w2, b2, wqkv, bqk, bvv, wl, bl, out):
    with ExitStack() as keep:
        def sb(name, shape, dt=F32, stack=keep):
            return stack.enter_context(nc.sbuf_tensor(name, shape, dt))

        def sem(name):
            return keep.enter_context(nc.semaphore(name))

        bank = keep.enter_context(nc.psum_tensor("bank", [P, 8, HALF], F32))
        xres = sb("xres", [P, B * T, P])
        xhat = sb("xhat", [P, T, P])
        xhat_r = sb("xhat_r", [P, T, P])
        xT = sb("xT", [P, S])
        ident = sb("ident", [P, P])
        stats = sb("stats", [P, T, 6])
        meanvar = sb("meanvar", [P, T, 2])
        rstd = sb("rstd", [P, T])
        half_var = sb("half_var", [P, T])
        varp = sb("varp", [P, T])
        newton = sb("newton", [P, T])
        magic = sb("magic", [P, T], I32)
        w1_sb = sb("w1_sb", [P, E, HID])
        w2_sb = sb("w2_sb", [P, E, HC, P])
        b1_sb = sb("b1_sb", [P, E * HC])
        b2_sb = sb("b2_sb", [P, E])
        wr_sb = sb("wr_sb", [P, E])
        before = sb("before", [P, P], BF16)
        ones = sb("ones", [P, P], BF16)
        rev = sb("rev", [P, E])
        rowbase = sb("rowbase", [P, B, E])
        bl_sb = sb("bl_sb", [P, P])
        bout_sb = sb("bout_sb", [P, P])
        xslots = nc.dram_tensor("xslots", [B * SLOTS, P], F32, kind="Internal").ap()
        yslots = nc.dram_tensor("yslots", [B * SLOTS, P], F32, kind="Internal").ap()

        load_x0 = sem("load_x0")
        load_x = sem("load_x")
        load_a = sem("load_a")
        load_f = sem("load_f")
        load_c = sem("load_c")
        consts = sem("consts")
        pool_step = sem("pool_step")
        dve_step = sem("dve_step")
        zeroed = sem("zeroed")
        ln_xhat = sem("ln_xhat")
        ln_tr = sem("ln_tr")
        ln_xT = sem("ln_xT")
        a_xproj, a_gproj, a_vproj, a_lktr = sem("a_xproj"), sem("a_gproj"), sem("a_vproj"), sem("a_lktr")
        a_sq, a_sl, a_kv, a_o, a_out = sem("a_sq"), sem("a_sl"), sem("a_kv"), sem("a_o"), sem("a_out")
        a_xs, a_gs, a_v, a_lkt, a_usq = sem("a_xs"), sem("a_gs"), sem("a_v"), sem("a_lkt"), sem("a_usq")
        a_feat, a_vbias, a_u, a_at = sem("a_feat"), sem("a_vbias"), sem("a_u"), sem("a_at")
        a_state, a_gated, a_res = sem("a_state"), sem("a_gated"), sem("a_res")
        f_lg, f_pos, f_str, f_h, f_y, f_ytr = (sem(n) for n in ("f_lg", "f_pos", "f_str", "f_h", "f_y", "f_ytr"))
        f_sub, f_exp, f_m, f_idx = sem("f_sub"), sem("f_exp"), sem("f_m"), sem("f_idx")
        f_xs, f_ha, f_hd, f_ya, f_ys = (sem(n) for n in ("f_xs", "f_ha", "f_hd", "f_ya", "f_ys"))
        f_sc, f_ld, f_st, f_ga, f_comb = (sem(n) for n in ("f_sc", "f_ld", "f_st", "f_ga", "f_comb"))
        c_stage = [sem("c_stage0"), sem("c_stage1")]
        c_proj, c_hi, c_pev, c_dup = (sem(n) for n in ("c_proj", "c_hi", "c_pev", "c_dup"))
        c_qk, c_max, c_exp, c_vs, c_av = (sem(n) for n in ("c_qk", "c_max", "c_exp", "c_vs", "c_av"))
        c_ctx, c_out, c_res = sem("c_ctx"), sem("c_out"), sem("c_res")
        stored = sem("stored")
        scaled = sem("scaled")
        waits = sem("waits")

        def hold(engine, s, value):
            engine.wait_ge(s, value)
            engine.sem_inc(waits, 1)

        class Steps:
            def __init__(self, engine, s):
                self.engine, self.sem, self.n = engine, s, 0

            def wait(self):
                self.engine.wait_ge(self.sem, self.n)

            def done(self, ins):
                self.n = self.n + 1
                ins.then_inc(self.sem, 1)

            def then(self, ins):
                self.done(ins)
                self.wait()

        per_row = {
            ln_xhat: T, ln_tr: T, ln_xT: 2,
            a_xproj: 2, a_gproj: 4, a_vproj: T, a_lktr: T, a_sq: T, a_sl: T, a_kv: T - 1, a_o: 2 * T, a_out: T,
            a_xs: 2, a_gs: 4, a_v: 4, a_lkt: 2, a_usq: 2, a_feat: 4, a_vbias: 4, a_u: 2, a_at: 2, a_state: T - 1,
            a_gated: 4, a_res: 2,
            f_lg: 1, f_pos: 1, f_str: ST, f_h: 2 * E, f_y: E, f_ytr: ST, f_sub: 1, f_exp: 1, f_m: 1, f_idx: 1,
            f_xs: 3, f_ha: E, f_hd: E, f_ya: E, f_ys: 3, f_ld: 16, f_st: 16, f_comb: 2 * T,
            c_stage[0]: 8 * PAIRS, c_stage[1]: 8 * PAIRS, c_proj: 6 * PAIRS, c_hi: 8 * PAIRS, c_pev: 6 * PAIRS, c_dup: 32 * PAIRS,
            c_qk: 2 * T * PAIRS, c_max: 2 * T * PAIRS, c_exp: 2 * T * PAIRS, c_vs: T * PAIRS, c_av: T * PAIRS,
            c_ctx: 2 * PAIRS, c_out: 2 * PAIRS, c_res: 2 * PAIRS,
        }

        def ln_vector(v, step, n, b, xh, bias=None):
            xb = xres[:, bass.ds(b * T, T), :]
            for t in range(T):
                step.done(nc.vector.bn_stats(stats[:, t, :], xres[:, bass.ds(b * T + t, 1), :].rearrange("p a c -> p (a c)")))
            hold(v, dve_step, step.n)
            for t in range(T):
                ins = nc.vector.bn_aggr(meanvar[:, t, :], stats[:, t, :])
            step.then(ins)
            step.then(nc.vector.tensor_scalar(varp[:], meanvar[:, :, 1], EPS, None, ALU.add))
            step.done(nc.vector.tensor_scalar(half_var[:], varp[:], -0.5, None, ALU.mult))
            step.then(nc.vector.tensor_scalar(newton[:].bitcast(I32), varp[:].bitcast(I32), 1, None, ALU.arith_shift_right))
            step.then(nc.vector.tensor_tensor(rstd[:].bitcast(I32), magic[:], newton[:].bitcast(I32), ALU.subtract))
            for _ in range(4):
                step.then(nc.vector.tensor_tensor(newton[:], rstd[:], rstd[:], ALU.mult))
                step.then(nc.vector.tensor_tensor(newton[:], newton[:], half_var[:], ALU.mult))
                step.then(nc.vector.scalar_tensor_tensor(out=rstd[:], in0=newton[:], scalar=1.5, in1=rstd[:],
                                                         op0=ALU.add, op1=ALU.mult))
            v.wait_ge(ln_tr, n * T)
            for t in range(T):
                nc.vector.tensor_scalar(xh[:, t, :], xres[:, bass.ds(b * T + t, 1), :].rearrange("p a c -> p (a c)"),
                                        meanvar[:, t, 0:1], rstd[:, t:t + 1], ALU.subtract, ALU.mult).then_inc(ln_xhat, 1)
            if bias is not None:
                v.wait_ge(ln_xhat, (n + 1) * T)
                step.done(nc.vector.tensor_tensor(xb, xb, bias[:].unsqueeze(1).to_broadcast([P, T, P]), ALU.add))

        def ln_tensor(pe, n, xh):
            for t in range(T):
                pe.wait_ge(ln_xhat, n * T + t + 1)
                nc.tensor.transpose(bank[:, t // 4, (t % 4) * P:(t % 4 + 1) * P], xh[:, t, :], ident[:]).then_inc(ln_tr, 1)

        def ln_scalar(a, n):
            for h in range(2):
                a.wait_ge(ln_tr, n * T + 4 * (h + 1))
                nc.scalar.activation(xT[:, h * HALF:(h + 1) * HALF], bank[:, h, :], ACT.Copy).then_inc(ln_xT, 1)

        def cols(i, n=P):
            return slice(i * n, (i + 1) * n)

        stage_f = keep
        def small(name, dt=F32):
            return sb(name, [P, T, E], dt, stack=stage_f)
        lg, ex, pr, eq, key, pr2, tmp = (small(n) for n in ("lg", "ex", "pr", "eq", "key", "pr2", "tmp"))
        oh = [small("oh1"), small("oh2")]
        chosen = small("chosen", BF16)
        rowmat, keepmat = small("rowmat"), small("keepmat")
        nmax, rsum, rinv, rk = (sb(n, [P, T], stack=stage_f) for n in ("nmax", "rsum", "rinv", "rk"))
        ptop = sb("ptop", [P, 2, T], stack=stage_f)
        kept = sb("kept", [P, 2, T], stack=stage_f)
        wtok = sb("wtok", [P, 2, T], stack=stage_f)
        wtok_ring = sb("wtok_ring", [P, B, 2 * T], stack=stage_f)
        rowf = sb("rowf", [P, 2, T], stack=stage_f)
        skip = sb("skip", [P, 2, T], stack=stage_f)
        row_g = sb("row_g", [P, 2, T], U32, stack=stage_f)
        row_ring = sb("row_ring", [P, B, 2 * T], U32, stack=stage_f)
        row_s = sb("row_s", [P, 2, T], U32, stack=stage_f)
        slots_sb = sb("slots_sb", [P, ST, P], stack=stage_f)
        xsT = sb("xsT", [P, SLOTS], stack=stage_f)
        hT = sb("hT", [P, 2, HC, CAP], stack=stage_f)
        yT = sb("yT", [P, SLOTS], stack=stage_f)
        yg = sb("yg", [P, 2, T, P], stack=stage_f)
        TR = [(2, 0, 4), (3, 4, 8), (4, 8, ST)]

        def over_e(t):
            return t.unsqueeze(2).to_broadcast([P, T, E])

        def route_tensor(pe, m, n):
            ln_tensor(pe, n, xhat_r)
            pe.wait_ge(ln_xT, 2 * n + 2)
            for t in range(T):
                ins = nc.tensor.matmul(bank[:, 0, t * E:(t + 1) * E], xT[:, cols(t)], wr_sb[:], start=True, stop=True)
            ins.then_inc(f_lg, 1)

        def positions(pe, m):
            pe.wait_ge(f_m, m + 1)
            pos = bank[:, 1, 0:T * E].rearrange("p (t e) -> p t e", e=E)
            nc.tensor.matmul(bank[:, 1, 0:T * E], before[:], chosen[:].rearrange("p t e -> p (t e)"), start=True, stop=False)
            for t in range(T - 1):
                ins = nc.tensor.matmul(pos[:, t + 1:T, :], ones[:], chosen[:, t:t + 1, :].to_broadcast([P, T - 1 - t, E]),
                                       start=False, stop=(t == T - 2))
            ins.then_inc(f_pos, 1)

        def experts_tensor(pe, m, between):
            pe.wait_ge(f_ld, 16 * (m + 1))
            for bk, lo, hi in TR:
                for i in range(lo, hi):
                    nc.tensor.transpose(bank[:, bk, cols(i - lo)], slots_sb[:, i, :], ident[:]).then_inc(f_str, 1)
            pe.wait_ge(f_xs, 3 * (m + 1))

            def up(e):
                if e >= 2:
                    pe.wait_ge(f_ha, E * m + e - 1)
                for c in range(HC):
                    ins = nc.tensor.matmul(bank[:, 2 + 2 * (e % 2) + c // 2, cols(c % 2, CAP)], w1_sb[:, e, cols(c)],
                                           xsT[:, cols(e, CAP)], start=True, stop=True)
                    if c % 2:
                        ins.then_inc(f_h, 1)

            def down(e):
                pe.wait_ge(f_ha, E * m + e + 1)
                if e >= 2:
                    pe.wait_ge(f_ya, E * m + e - 1)
                for c in range(HC):
                    ins = nc.tensor.matmul(bank[:, 6 + e % 2, 0:CAP], w2_sb[:, e, c, :], hT[:, e % 2, c, :],
                                           start=(c == 0), stop=(c == HC - 1))
                ins.then_inc(f_y, 1)

            up(0)
            for e in range(1, E):
                up(e)
                down(e - 1)
                if e == 3:
                    between()
            down(E - 1)
            pe.wait_ge(f_ya, E * (m + 1))
            for bk, lo, hi in TR:
                for i in range(lo, hi):
                    nc.tensor.transpose(bank[:, bk, cols(i - lo)], yT[:, cols(i)], ident[:]).then_inc(f_ytr, 1)

        def behind_tensor(pe, m, n, experts):
            route_tensor(pe, m, n)
            if experts:
                experts_tensor(pe, m - 1, lambda: positions(pe, m))
            else:
                positions(pe, m)

        def route_scalar(a, m, n):
            ln_scalar(a, n)
            a.wait_ge(f_sub, m + 1)
            nc.scalar.activation(ex[:], lg[:], ACT.Exp).then_inc(f_exp, 1)

        def experts_scalar(a, m):
            for bk, lo, hi in TR:
                a.wait_ge(f_str, ST * m + hi)
                nc.scalar.activation(xsT[:, lo * P:hi * P], bank[:, bk, 0:(hi - lo) * P], ACT.Copy).then_inc(f_xs, 1)

            def hidden(e):
                if e >= 2:
                    a.wait_ge(f_y, E * m + e - 1)
                for c in range(HC):
                    if c % 2 == 0:
                        a.wait_ge(f_h, 2 * E * m + 2 * e + c // 2 + 1)
                    ins = nc.scalar.activation(hT[:, e % 2, c, :], bank[:, 2 + 2 * (e % 2) + c // 2, cols(c % 2, CAP)],
                                               ACT.Relu, bias=b1_sb[:, e * HC + c:e * HC + c + 1])
                ins.then_inc(f_ha, 1)

            def answer(e):
                a.wait_ge(f_y, E * m + e + 1)
                nc.scalar.activation(yT[:, cols(e, CAP)], bank[:, 6 + e % 2, 0:CAP], ACT.Identity,
                                     bias=b2_sb[:, e:e + 1]).then_inc(f_ya, 1)

            hidden(0)
            for e in range(1, E):
                hidden(e)
                answer(e - 1)
            answer(E - 1)
            for bk, lo, hi in TR:
                a.wait_ge(f_ytr, ST * m + hi)
                nc.scalar.activation(slots_sb[:, lo:hi, :], bank[:, bk, 0:(hi - lo) * P].rearrange("p (t c) -> p t c", c=P),
                                     ACT.Copy).then_inc(f_ys, 1)

        def route_vector(v, step, m, n, b):
            hold(v, f_ld, 16 * m)
            ln_vector(v, step, n, b, xhat_r)
            v.wait_ge(f_lg, m + 1)
            logits = bank[:, 0, 0:T * E].rearrange("p (t e) -> p t e", e=E)
            step.then(nc.vector.tensor_reduce(nmax[:], logits, X_AXIS, ALU.max))
            nc.vector.tensor_tensor(lg[:], logits, over_e(nmax[:]), ALU.subtract).then_inc(f_sub, 1)
            v.wait_ge(f_exp, m + 1)
            step.then(nc.vector.tensor_reduce(rsum[:], ex[:], X_AXIS, ALU.add))
            step.then(nc.vector.reciprocal(rinv[:], rsum[:]))
            step.then(nc.vector.tensor_tensor(pr[:], ex[:], over_e(rinv[:]), ALU.mult))
            p_now = pr
            for k in range(2):
                step.then(nc.vector.tensor_reduce(ptop[:, k, :], p_now[:], X_AXIS, ALU.max))
                step.then(nc.vector.tensor_tensor(eq[:], p_now[:], over_e(ptop[:, k, :]), ALU.is_equal))
                step.then(nc.vector.tensor_tensor(key[:], eq[:], rev[:].unsqueeze(1).to_broadcast([P, T, E]), ALU.mult))
                step.then(nc.vector.tensor_reduce(rk[:], key[:], X_AXIS, ALU.max))
                step.then(nc.vector.tensor_tensor(oh[k][:], key[:], over_e(rk[:]), ALU.is_equal))
                if k == 0:
                    step.then(nc.vector.scalar_tensor_tensor(out=pr2[:], in0=oh[0][:], scalar=-2.0, in1=pr[:],
                                                             op0=ALU.mult, op1=ALU.add))
                    p_now = pr2
            nc.vector.tensor_tensor(chosen[:], oh[0][:], oh[1][:], ALU.add).then_inc(f_m, 1)
            v.wait_ge(f_pos, m + 1)
            pos = bank[:, 1, 0:T * E].rearrange("p (t e) -> p t e", e=E)
            step.done(nc.vector.tensor_scalar(keepmat[:], pos, float(CAP), None, ALU.is_lt))
            step.then(nc.vector.tensor_scalar(tmp[:], pos, float(CAP - 1), None, ALU.min))
            step.then(nc.vector.tensor_tensor(rowmat[:], tmp[:],
                                              rowbase[:, bass.ds(b, 1), :].to_broadcast([P, T, E]), ALU.add))
            for k in range(2):
                step.then(nc.vector.tensor_tensor(tmp[:], oh[k][:], rowmat[:], ALU.mult))
                step.then(nc.vector.tensor_reduce(rowf[:, k, :], tmp[:], X_AXIS, ALU.add))
                step.then(nc.vector.tensor_tensor(tmp[:], oh[k][:], keepmat[:], ALU.mult))
                step.then(nc.vector.tensor_reduce(kept[:, k, :], tmp[:], X_AXIS, ALU.add))
            step.done(nc.vector.tensor_copy(row_ring[:, bass.ds(b, 1), :].rearrange("p a c -> p (a c)"),
                                            rowf[:].rearrange("p k t -> p (k t)")))
            step.then(nc.vector.tensor_scalar(skip[:], kept[:], -SKIPPED, SKIPPED, ALU.mult, ALU.add))
            step.done(nc.vector.tensor_tensor(wtok_ring[:, bass.ds(b, 1), :].rearrange("p a c -> p (a c)"),
                                              ptop[:].rearrange("p k t -> p (k t)"), kept[:].rearrange("p k t -> p (k t)"), ALU.mult))
            nc.vector.tensor_tensor(row_s[:], rowf[:], skip[:], ALU.add).then_inc(f_idx, 1)

        ROUTE_STEPS = 4 + 5 + 1 + 5 + 3 + 8 + 3
        LN_STEPS = T + 1 + 4 + 12

        def combine_vector(v, step, m, b):
            step.then(nc.vector.tensor_copy(wtok[:].rearrange("p k t -> p (k t)"),
                                            wtok_ring[:, bass.ds(b, 1), :].rearrange("p a c -> p (a c)")))
            v.wait_ge(f_ga, 256 * m)
            for k in range(2):
                for t in range(T):
                    xr = xres[:, bass.ds(b * T + t, 1), :].rearrange("p a c -> p (a c)")
                    ins = nc.vector.scalar_tensor_tensor(out=xr, in0=yg[:, k, t, :], scalar=wtok[:, k, t:t + 1], in1=xr,
                                                         op0=ALU.mult, op1=ALU.add)
                    ins.then_inc(f_comb, 1)
                hold(v, f_comb, 2 * T * m + T * (k + 1))

        def scatter(p, m):
            hold(p, f_idx, m + 1)
            for k in range(2):
                for t in range(T):
                    nc.gpsimd.indirect_dma_start(out=xslots[:, :], out_offset=bass.IndirectOffsetOnAxis(ap=row_s[:, k, t:t + 1], axis=0),
                                                 in_=xhat_r[:, t, :], in_offset=None,
                                                 bounds_check=B * SLOTS - 1, oob_is_err=False).then_inc(f_sc, 16)

        def gather(p, step, m, b):
            hold(p, f_comb, 2 * T * m)
            step.then(nc.gpsimd.tensor_copy(row_g[:].rearrange("p k t -> p (k t)"),
                                            row_ring[:, bass.ds(b, 1), :].rearrange("p a c -> p (a c)")))
            hold(p, f_st, 16 * (m + 1))
            for k in range(2):
                for t in range(T):
                    nc.gpsimd.indirect_dma_start(out=yg[:, k, t, :], out_offset=None, in_=yslots[:, :],
                                                 in_offset=bass.IndirectOffsetOnAxis(ap=row_g[:, k, t:t + 1], axis=0),
                                                 bounds_check=B * SLOTS - 1, oob_is_err=False).then_inc(f_ga, 16)

        def load_slots(sp, m, b):
            hold(sp, f_st, 16 * m)
            hold(sp, f_sc, 256 * m)
            sp.dma_start(slots_sb[:], xslots[bass.ds(b * SLOTS, SLOTS), :].rearrange("(i p) c -> p i c", p=P)).then_inc(f_ld, 16)

        def store_slots(sp, m, b):
            hold(sp, f_ys, 3 * (m + 1))
            sp.dma_start(yslots[bass.ds(b * SLOTS, SLOTS), :].rearrange("(i p) c -> p i c", p=P), slots_sb[:]).then_inc(f_st, 16)

        stage_a = ExitStack()
        wv_sb = sb("wv_sb", [P, INNER], stack=stage_a)
        wg_sb = sb("wg_sb", [P, INNER], stack=stage_a)
        win_sb = sb("win_sb", [P, P], stack=stage_a)
        wout_sb = sb("wout_sb", [P, EH, P], stack=stage_a)
        bv_sb = sb("bv_sb", [P, INNER], stack=stage_a)
        ca = sb("ca", [P, 11], stack=stage_a)
        m_quad = sb("m_quad", [P, P], stack=stage_a)
        m_lin = sb("m_lin", [P, P], stack=stage_a)
        base = sb("base", [P, S], stack=stage_a)
        qqT, qkT, lqT, lkT = (sb(n, [P, S], stack=stage_a) for n in ("qqT", "qkT", "lqT", "lkT"))
        gateT = sb("gateT", [P, EH, S], stack=stage_a)
        vpre = sb("vpre", [P, T, INNER], stack=stage_a)
        vact = sb("vact", [P, T, INNER], stack=stage_a)
        lk = sb("lk", [P, T, P], stack=stage_a)
        relu_m = sb("relu_m", [P, S], stack=stage_a)
        relu_sq = sb("relu_sq", [P, S], stack=stage_a)
        lin_m = sb("lin_m", [P, S], stack=stage_a)
        attnT = sb("attnT", [P, S], stack=stage_a)
        state = sb("state", [P, T, INNER], stack=stage_a)
        gatedT = sb("gatedT", [P, EH, S], stack=stage_a)
        KV_BANK = [2, 2, 3, 3, 4, 4, 5]

        def a_tensor(pe, r, n):
            ln_tensor(pe, n, xhat)
            pe.wait_ge(f_ys, 3 * max(r - 1, 1) if isinstance(r, int) else 3 * (r - 1))
            for h in range(2):
                pe.wait_ge(ln_xT, 2 * n + h + 1)
                nc.tensor.matmul(bank[:, 2 + h, :], win_sb[:], xT[:, cols(h, HALF)], start=True, stop=True).then_inc(a_xproj, 1)
            for e in range(EH):
                for h in range(2):
                    nc.tensor.matmul(bank[:, 4 + 2 * e + h, :], wg_sb[:, cols(e)], xT[:, cols(h, HALF)],
                                     start=True, stop=True).then_inc(a_gproj, 1)
            for t in range(T):
                if t == 4:
                    pe.wait_ge(a_xs, 2 * r + 2)
                nc.tensor.matmul(bank[:, t // 2, cols(t % 2, INNER)], xT[:, cols(t)], wv_sb[:],
                                 start=True, stop=True).then_inc(a_vproj, 1)
            pe.wait_ge(a_gs, 4 * r + 2)
            pe.wait_ge(a_feat, 4 * r + 1)
            for t in range(T):
                nc.tensor.transpose(bank[:, 4 + t // 4, cols(t % 4)], lkT[:, cols(t)], ident[:]).then_inc(a_lktr, 1)
            pe.wait_ge(a_gs, 4 * r + 4)
            pe.wait_ge(a_feat, 4 * r + 3)
            for t in range(T):
                nc.tensor.matmul(bank[:, 6 + t // 4, cols(t % 4)], qkT[:, cols(t)], qqT[:, cols(t)],
                                 start=True, stop=True).then_inc(a_sq, 1)
            pe.wait_ge(a_feat, 4 * r + 4)
            pe.wait_ge(a_vbias, 4 * r + 2)
            for t in range(T):
                nc.tensor.matmul(bank[:, t // 4, cols(t % 4)], lkT[:, cols(t)], lqT[:, cols(t)],
                                 start=True, stop=True).then_inc(a_sl, 1)
            pe.wait_ge(a_v, 4 * r + 4)
            pe.wait_ge(a_lkt, 2 * r + 2)
            for t in range(T - 1):
                nc.tensor.matmul(bank[:, KV_BANK[t], cols(t % 2, INNER)], lk[:, t, :], vact[:, t, :],
                                 start=True, stop=True).then_inc(a_kv, 1)
            pe.wait_ge(a_at, 2 * r + 2)
            for e in range(EH):
                for t in range(T):
                    o = bank[:, (6 if e == 0 else 0) + t // 4, cols(t % 4)]
                    ins = nc.tensor.matmul(o, vact[:, t, cols(e)], attnT[:, cols(t)], start=True, stop=(t == 0))
                    if t > 0:
                        if e == 0:
                            pe.wait_ge(a_state, 7 * r + t)
                        ins = nc.tensor.matmul(o, state[:, t, cols(e)], lqT[:, cols(t)], start=False, stop=True)
                    ins.then_inc(a_o, 1)
            pe.wait_ge(a_gated, 4 * r + 4)
            for t in range(T):
                for e in range(EH):
                    ins = nc.tensor.matmul(bank[:, 2 + t // 4, cols(t % 4)], gatedT[:, e, cols(t)], wout_sb[:, e, :],
                                           start=(e == 0), stop=(e == EH - 1))
                ins.then_inc(a_out, 1)

        def a_scalar(a, r, n):
            ln_scalar(a, n)
            for h in range(2):
                a.wait_ge(a_xproj, 2 * r + h + 1)
                nc.scalar.activation(base[:, cols(h, HALF)], bank[:, 2 + h, :], ACT.Silu, bias=ca[:, 2:3]).then_inc(a_xs, 1)
            for e in range(EH):
                for h in range(2):
                    a.wait_ge(a_gproj, 4 * r + 2 * e + h + 1)
                    nc.scalar.activation(gateT[:, e, cols(h, HALF)], bank[:, 4 + 2 * e + h, :], ACT.Silu,
                                         bias=ca[:, e:e + 1]).then_inc(a_gs, 1)
            for k in range(4):
                a.wait_ge(a_vbias, 4 * r + k + 1)
                nc.scalar.activation(vact[:, 2 * k:2 * k + 2, :], vpre[:, 2 * k:2 * k + 2, :], ACT.Silu).then_inc(a_v, 1)
            for h in range(2):
                a.wait_ge(a_lktr, T * r + 4 * (h + 1))
                nc.scalar.activation(lk[:, 4 * h:4 * h + 4, :], bank[:, 4 + h, :].rearrange("p (t c) -> p t c", c=P),
                                     ACT.Copy).then_inc(a_lkt, 1)
            for h in range(2):
                a.wait_ge(a_u, 2 * r + h + 1)
                nc.scalar.activation(relu_sq[:, cols(h, HALF)], relu_m[:, cols(h, HALF)], ACT.Square).then_inc(a_usq, 1)

        def a_vector(v, step, r, n, b):
            ln_vector(v, step, n, b, xhat, bout_sb)
            v.wait_ge(a_xs, 2 * r + 2)
            for dst, c in ((lkT, 9), (qkT, 5), (qqT, 3), (lqT, 7)):
                nc.vector.tensor_scalar(dst[:], base[:], ca[:, c:c + 1], ca[:, c + 1:c + 2], ALU.mult, ALU.add).then_inc(a_feat, 1)
            for k in range(4):
                v.wait_ge(a_vproj, T * r + 2 * (k + 1))
                nc.vector.tensor_tensor(vpre[:, 2 * k:2 * k + 2, :], bank[:, k, :].rearrange("p (t c) -> p t c", c=INNER),
                                        bv_sb[:].unsqueeze(1).to_broadcast([P, 2, INNER]), ALU.add).then_inc(a_vbias, 1)
            for h in range(2):
                v.wait_ge(a_sq, T * r + 4 * (h + 1))
                nc.vector.scalar_tensor_tensor(
                    out=relu_m[:, cols(h, HALF)].rearrange("p (t c) -> p t c", c=P),
                    in0=bank[:, 6 + h, :].rearrange("p (t c) -> p t c", c=P), scalar=0.0,
                    in1=m_quad[:].unsqueeze(1).to_broadcast([P, 4, P]), op0=ALU.max, op1=ALU.mult).then_inc(a_u, 1)
            for h in range(2):
                v.wait_ge(a_sl, T * r + 4 * (h + 1))
                step.done(nc.vector.tensor_tensor(
                    lin_m[:, cols(h, HALF)].rearrange("p (t c) -> p t c", c=P),
                    bank[:, h, :].rearrange("p (t c) -> p t c", c=P),
                    m_lin[:].unsqueeze(1).to_broadcast([P, 4, P]), ALU.mult))
            step.wait()
            for h in range(2):
                v.wait_ge(a_usq, 2 * r + h + 1)
                nc.vector.tensor_tensor(attnT[:, cols(h, HALF)], relu_sq[:, cols(h, HALF)], lin_m[:, cols(h, HALF)],
                                        ALU.add).then_inc(a_at, 1)
            for t in range(1, T):
                v.wait_ge(a_kv, 7 * r + min(t + t % 2, T - 1))
                kv = bank[:, KV_BANK[t - 1], cols((t - 1) % 2, INNER)]
                if t == 1:
                    nc.vector.tensor_copy(state[:, t, :], kv).then_inc(a_state, 1)
                else:
                    v.wait_ge(a_state, 7 * r + t - 1)
                    nc.vector.tensor_tensor(state[:, t, :], kv, state[:, t - 1, :], ALU.add).then_inc(a_state, 1)
            for e in range(EH):
                for h in range(2):
                    v.wait_ge(a_o, 2 * T * r + T * e + 4 * (h + 1))
                    nc.vector.tensor_tensor(gatedT[:, e, cols(h, HALF)], bank[:, (6 if e == 0 else 0) + h, :],
                                            gateT[:, e, cols(h, HALF)], ALU.mult).then_inc(a_gated, 1)
            for h in range(2):
                v.wait_ge(a_out, T * r + 4 * (h + 1))
                xr = xres[:, bass.ds(b * T + 4 * h, 4), :]
                nc.vector.tensor_tensor(xr, bank[:, 2 + h, :].rearrange("p (t c) -> p t c", c=P), xr, ALU.add).then_inc(a_res, 1)
            hold(v, a_res, 2 * r + 2)
        stage_a.close()

        stage_c = ExitStack()
        wall = sb("wall", [P, PAIRS, WCOLS], stack=stage_c)
        wl_sb = sb("wl_sb", [P, PAIRS, P], stack=stage_c)
        ws = [sb(f"ws{i}", [P, WCOLS], stack=stage_c) for i in range(2)]
        qst = [[sb(f"q{i}{h}", [P, 2, S], F32R, stack=stage_c) for h in range(2)] for i in range(2)]
        kst = [[sb(f"k{i}{h}", [P, S], F32R, stack=stage_c) for h in range(2)] for i in range(2)]
        vst = [sb(f"v{i}", [P, T, P], stack=stage_c) for i in range(2)]
        prob = [[sb(f"prob{i}{h}", [P, S], stack=stage_c) for h in range(2)] for i in range(2)]
        vsc = [sb(f"vsc{i}", [P, P], stack=stage_c) for i in range(2)]
        nmx = sb("nmx", [P, 4], stack=stage_c)
        zsum = sb("zsum", [P, 4], stack=stage_c)
        zinv = sb("zinv", [P, 4], stack=stage_c)
        ctxT = sb("ctxT", [P, S], stack=stage_c)
        SC = [(0, 1), (2, 3)]
        CX = (4, 5)
        PJ = (6, 7)
        SPAN = 2 * T
        LEAD = 2

        def rows(h):
            return slice(h * HD, (h + 1) * HD)

        def project(pe, par, pi, k):
            w = ws[par]
            if k == 0:
                pe.wait_ge(c_stage[par], 8 * (pi - par + 2))
            if k < 2:
                pe.wait_ge(c_res, 2 * (pi - 3) + k + 1)
            else:
                pe.wait_ge(c_pev, 6 * pi + k - 1)
            if k < 4:
                ins = nc.tensor.matmul(bank[:, PJ[k % 2], :], w[:, (WQ if k < 2 else WK):(WQ if k < 2 else WK) + P],
                                       xT[:, cols(k % 2, HALF)], start=True, stop=True)
            else:
                for t in range(4):
                    ins = nc.tensor.matmul(bank[:, PJ[k % 2], cols(t)], xT[:, cols(4 * (k - 4) + t)], w[:, WV:WV + P],
                                           start=True, stop=True)
            ins.then_inc(c_proj, 1)

        def out_tensor(pe, pi, pair_row, n, last):
            if n == 0:
                pe.wait_ge(c_ctx, 2 * (pi + 1))
            if last:
                pe.wait_ge(c_res, 2 * pi - 1 + n)
            else:
                pe.wait_ge(c_pev, 6 * (pi + 3) - 1 + n)
            for t in range(4):
                ins = nc.tensor.matmul(bank[:, PJ[n], cols(t)], ctxT[:, cols(4 * n + t)],
                                       wl_sb[:, bass.ds(pair_row, 1), :].rearrange("p a c -> p (a c)"), start=True, stop=True)
            ins.then_inc(c_out, 1)

        def out_vector(v, pi, b, n):
            v.wait_ge(c_out, 2 * pi + n + 1)
            if n == 0:
                v.wait_ge(c_res, 2 * pi)
            xr = xres[:, bass.ds(b * T + 4 * n, 4), :]
            nc.vector.tensor_tensor(xr, bank[:, PJ[n], :].rearrange("p (t c) -> p t c", c=P), xr, ALU.add).then_inc(c_res, 1)

        def proj_hi(a, par, pr_i, k):
            w = ws[par]
            a.wait_ge(c_proj, 6 * pr_i + k + 1)
            for h in range(2):
                r = rows(h)
                dst = qst[par][h][r, 0, cols(k % 2, HALF)] if k < 2 else kst[par][h][r, cols(k % 2, HALF)]
                bias = w[r, BQ:BQ + 1] if k < 2 else w[r, BK:BK + 1]
                nc.scalar.activation(dst, bank[r, PJ[k % 2], :], ACT.Identity, bias=bias).then_inc(c_hi, 1)

        def proj_lo(v, par, pr_i, k):
            w = ws[par]
            if k >= 4:
                v.wait_ge(c_proj, 6 * pr_i + k + 1)
                nc.vector.tensor_tensor(vst[par][:, 4 * (k - 4):4 * (k - 3), :],
                                        bank[:, PJ[k % 2], :].rearrange("p (t c) -> p t c", c=P),
                                        w[:, BV:BV + P].unsqueeze(1).to_broadcast([P, 4, P]), ALU.add).then_inc(c_pev, 1)
                return
            for h in range(2):
                r, o = rows(h), rows(1 - h)
                v.wait_ge(c_hi, 8 * pr_i + 2 * k + h + 1)
                if k < 2:
                    hi, lo = qst[par][h][r, 0, cols(k, HALF)], qst[par][h][r, 1, cols(k, HALF)]
                    bias = w[r, BQ:BQ + 1]
                else:
                    hi, lo = kst[par][h][r, cols(k - 2, HALF)], kst[par][h][o, cols(k - 2, HALF)]
                    bias = w[r, BK:BK + 1]
                ins = nc.vector.scalar_tensor_tensor(out=lo, in0=bank[r, PJ[k % 2], :], scalar=bias, in1=hi.bitcast(F32),
                                                     op0=ALU.add, op1=ALU.subtract)
            ins.then_inc(c_pev, 1)

        def q_copy(sp, par, pr_i):
            hold(sp, c_pev, 6 * pr_i + 2)
            for h in range(2):
                src = qst[par][h][rows(h), :, :].bitcast(F32)
                dst = qst[par][h][rows(1 - h), :, :].bitcast(F32)
                sp.dma_start(dst, src).then_inc(c_dup, 16)

        def scores(pe, par, j, g, first=False):
            for h in range(2):
                if not first:
                    pe.wait_ge(c_exp, 2 * g + h - 1)
                for n in range(2):
                    o = bank[:, SC[h][n], :]
                    kk = kst[par][h][:, cols(j)]
                    nc.tensor.matmul(o, kk, qst[par][h][:, 0, cols(n, HALF)], start=True, stop=False)
                    ins = nc.tensor.matmul(o, kk, qst[par][h][:, 1, cols(n, HALF)], start=False, stop=True)
                ins.then_inc(c_qk, 1)

        def context(pe, j, g, pr_i):
            s = j % 2
            if j == 0:
                pe.wait_ge(c_ctx, 2 * pr_i)
            pe.wait_ge(c_vs, g + 1)
            for n in range(2):
                for h in range(2):
                    ins = nc.tensor.matmul(bank[rows(h), CX[n], :], vsc[s][:, rows(h)], prob[s][h][:, cols(n, HALF)],
                                           start=(j == 0), stop=(j == T - 1))
            ins.then_inc(c_av, 1)

        def score_max(v, g, s):
            for h in range(2):
                v.wait_ge(c_qk, 2 * g + h + 1)
                nc.vector.tensor_reduce(nmx[:, 2 * s + h:2 * s + h + 1], bank[:, SC[h][0]:SC[h][0] + 2, :],
                                        mybir.AxisListType.XY, ALU.max, negate=True).then_inc(c_max, 1)

        def score_exp(a, g, s):
            for h in range(2):
                a.wait_ge(c_max, 2 * g + h + 1)
                nc.scalar.activation(prob[s][h][:].rearrange("p (n c) -> p n c", c=HALF), bank[:, SC[h][0]:SC[h][0] + 2, :],
                                     ACT.Exp, bias=nmx[:, 2 * s + h:2 * s + h + 1],
                                     accum_out=zsum[:, 2 * s + h:2 * s + h + 1]).then_inc(c_exp, 1)

        def scale_v(v, step, par, j, g):
            s = j % 2
            v.wait_ge(c_exp, 2 * g + 2)
            step.then(nc.vector.reciprocal(zinv[:, 2 * s:2 * s + 2], zsum[:, 2 * s:2 * s + 2]))
            nc.vector.tensor_tensor(vsc[s][:].rearrange("p (h c) -> p h c", c=HD),
                                    vst[par][:, j, :].rearrange("p (h c) -> p h c", c=HD),
                                    zinv[:, 2 * s:2 * s + 2].unsqueeze(2).to_broadcast([P, 2, HD]), ALU.mult).then_inc(c_vs, 1)

        def steps_of(g0, pair0, last):
            for s in range(SPAN):
                yield s, s // T, s % T, g0 + s, pair0 + s // T

        def c_body_tensor(pe, g0, pair0, pair_row, first, last):
            for s, par, j, g, pi in steps_of(g0, pair0, last):
                if j < 6 and not (last and par == 1):
                    project(pe, 1 - par, pi + 1, j)
                if j >= 6 and not (first and par == 0):
                    out_tensor(pe, pi - 1, pair_row + par - 1, j - 6, last and par == 1)
                if j > 0:
                    context(pe, j, g, pi)
                if not (last and s + LEAD >= SPAN):
                    j2, par2 = (j + LEAD) % T, (par + (j + LEAD) // T) % 2
                    if j2 == 0:
                        pe.wait_ge(c_dup, 32 * (pi + 2))
                        pe.wait_ge(c_pev, 6 * (pi + 1) + 4)
                    scores(pe, par2, j2, g + LEAD)
                if j == 0:
                    context(pe, j, g, pi)

        def ctx_evac(a, g, pi):
            a.wait_ge(c_av, g + 1)
            a.wait_ge(c_out, 2 * pi)
            for n in range(2):
                nc.scalar.activation(ctxT[:, cols(n, HALF)], bank[:, CX[n], :], ACT.Copy).then_inc(c_ctx, 1)

        def c_body_scalar(a, g0, pair0, last):
            for s, par, j, g, pi in steps_of(g0, pair0, last):
                if j < 4 and not (last and par == 1):
                    proj_hi(a, 1 - par, pi + 1, j)
                if not (last and s + LEAD >= SPAN):
                    if j == 0:
                        a.wait_ge(c_av, g + 1)
                    score_exp(a, g + LEAD, s % 2)
                if j == T - 1:
                    ctx_evac(a, g, pi)

        def c_body_vector(v, step, g0, pair0, b, first, last):
            for s, par, j, g, pi in steps_of(g0, pair0, last):
                if j < 6 and not (last and par == 1):
                    proj_lo(v, 1 - par, pi + 1, j)
                if j >= 6 and not (first and par == 0):
                    out_vector(v, pi - 1, b, j - 6)
                if not (last and s + 1 >= SPAN):
                    if (last and s + LEAD >= SPAN) or j == 0:
                        v.wait_ge(c_av, g)
                    scale_v(v, step, (par + (j + 1) // T) % 2, (j + 1) % T, g + 1)
                if not (last and s + LEAD >= SPAN):
                    score_max(v, g + LEAD, s % 2)

        MIDDLE = PAIRS // 2 - 2

        def c_tensor(pe, r, n):
            ln_tensor(pe, n, xhat)
            pe.wait_ge(ln_xT, 2 * n + 2)
            pe.wait_ge(f_ys, 3 * (r + B - 1))
            g0, p0 = PAIRS * T * r, PAIRS * r
            for k in range(6):
                project(pe, 0, p0, k)
            pe.wait_ge(c_dup, 32 * (p0 + 1))
            pe.wait_ge(c_pev, 6 * p0 + 4)
            scores(pe, 0, 0, g0, first=True)
            scores(pe, 0, 1, g0 + 1)
            c_body_tensor(pe, g0, p0, 0, True, False)
            with pe.Fori(1, 1 + MIDDLE) as it:
                c_body_tensor(pe, g0 + SPAN * it, p0 + 2 * it, 2 * it, False, False)
            it = 1 + MIDDLE
            c_body_tensor(pe, g0 + SPAN * it, p0 + 2 * it, 2 * it, False, True)
            for h in range(2):
                out_tensor(pe, p0 + PAIRS - 1, PAIRS - 1, h, True)

        def c_scalar(a, r, n):
            ln_scalar(a, n)
            g0, p0 = PAIRS * T * r, PAIRS * r
            for k in range(4):
                proj_hi(a, 0, p0, k)
            for j in range(2):
                score_exp(a, g0 + j, j)
            with a.Fori(0, 1 + MIDDLE) as it:
                c_body_scalar(a, g0 + SPAN * it, p0 + 2 * it, False)
            it = 1 + MIDDLE
            c_body_scalar(a, g0 + SPAN * it, p0 + 2 * it, True)

        def c_vector(v, step, r, n, b):
            ln_vector(v, step, n, b, xhat, bl_sb)
            g0, p0 = PAIRS * T * r, PAIRS * r
            for k in range(6):
                proj_lo(v, 0, p0, k)
            for j in range(2):
                score_max(v, g0 + j, j)
            scale_v(v, step, 0, 0, g0)
            begin = step.n
            c_body_vector(v, step, g0, p0, b, True, False)
            with v.Fori(1, 1 + MIDDLE) as it:
                step.n = begin + SPAN * it
                c_body_vector(v, step, g0 + SPAN * it, p0 + 2 * it, b, False, False)
            it = 1 + MIDDLE
            step.n = begin + SPAN * it
            c_body_vector(v, step, g0 + SPAN * it, p0 + 2 * it, b, False, True)
            for h in range(2):
                out_vector(v, p0 + PAIRS - 1, b, h)
            hold(v, c_res, 2 * (p0 + PAIRS))

        def stage_pair(sp, pi, pair_row, par):
            hold(sp, c_pev, 6 * (pi - 1))
            sp.dma_start(ws[par][:], wall[:, bass.ds(pair_row, 1), :].rearrange("p a c -> p (a c)")).then_inc(c_stage[par], 16)

        def c_sync(sp, r, pair_loads):
            p0 = PAIRS * r
            stage_pair(sp, p0, 0, 0)
            stage_pair(sp, p0 + 1, 1, 1)
            q_copy(sp, 0, p0)
            q_copy(sp, 1, p0 + 1)
            pair_loads()
            with sp.Fori(1, PAIRS // 2) as it:
                for par in range(2):
                    stage_pair(sp, p0 + 2 * it + par, 2 * it + par, par)
                    q_copy(sp, par, p0 + 2 * it + par)
        stage_c.close()

        block = keep.enter_context(nc.Block())
        ITER_A = [0, 1]

        @block.sync
        def _(sp):
            xv = x.rearrange("(t p) c -> p t c", p=P)
            sp.dma_start(xres[:, 0:T, :], xv[:, 0:T, :]).then_inc(load_x0, 16)
            for dst, src in ((win_sb, win), (ca, cols_a), (wg_sb, wg), (wv_sb, wv)):
                sp.dma_start(dst[:], src).then_inc(load_a, 16)
            sp.dma_start(bout_sb[:], bout.partition_broadcast(P)).then_inc(load_a, 16)
            sp.dma_start(bv_sb[:], bv.partition_broadcast(P)).then_inc(load_a, 16)
            sp.dma_start(wout_sb[:], wout.rearrange("(e p) c -> p e c", p=P)).then_inc(load_a, 16)
            sp.dma_start(xres[:, T:, :], xv[:, T:, :]).then_inc(load_x, 16)
            sp.dma_start(wr_sb[:], wr).then_inc(load_f, 16)
            sp.dma_start(bl_sb[:], bl.partition_broadcast(P)).then_inc(load_f, 16)
            sp.dma_start(b1_sb[:], b1).then_inc(load_f, 16)
            sp.dma_start(b2_sb[:], b2).then_inc(load_f, 16)
            sp.wait_ge(zeroed, ZEROED)
            sp.dma_start(w1_sb[:], w1.rearrange("e p h -> p e h")).then_inc(load_f, 16)
            sp.dma_start(w2_sb[:], w2.rearrange("e (c p) n -> p e c n", p=P)).then_inc(load_f, 16)
            load_slots(sp, 1, 0)
            store_slots(sp, 1, 0)
            with sp.Fori(2, B) as b:
                load_slots(sp, b, b - 1)
                store_slots(sp, b, b - 1)
            sp.wait_ge(a_res, 2 * (B + 1))
            sp.dma_start(wall[:, :, 0:3 * P], wqkv).then_inc(load_c, 16)
            sp.dma_start(wall[:, :, BQ:BQ + 2], bqk).then_inc(load_c, 16)
            sp.dma_start(wall[:, :, BV:BV + P], bvv.partition_broadcast(P)).then_inc(load_c, 16)
            sp.dma_start(wl_sb[:], wl).then_inc(load_c, 16)
            sp.wait_ge(scaled, 1)
            with sp.Fori(0, B) as b:
                c_sync(sp, b + 1, lambda: load_slots(sp, B + b, (b + B - 1) % B))
                store_slots(sp, B + b, (b + B - 1) % B)
            load_slots(sp, 2 * B, B - 1)
            for b in range(B):
                if b == B - 2:
                    store_slots(sp, 2 * B, B - 1)
                sp.wait_ge(f_comb, 2 * T * (B + b + 2))
                sp.dma_start(out[b * S:(b + 1) * S, :].rearrange("(t p) c -> p t c", p=P),
                             xres[:, b * T:(b + 1) * T, :]).then_inc(stored, 16)
            sp.wait_ge(stored, 16 * B)

        @block.gpsimd
        def _(p):
            step = Steps(p, pool_step)
            step.done(nc.gpsimd.memset(xhat_r[:], 0.0))
            step.done(nc.gpsimd.memset(magic[:], 0x5f3759df))
            step.done(nc.gpsimd.memset(ident[:], 1.0))
            step.done(nc.gpsimd.memset(before[:], 1.0))
            step.done(nc.gpsimd.memset(ones[:], 1.0))
            step.done(nc.gpsimd.memset(m_quad[:], 0.0))
            step.done(nc.gpsimd.memset(m_lin[:], 0.0))
            step.done(nc.gpsimd.iota(rev[:], [[-1, E]], base=E, channel_multiplier=0, allow_small_or_imprecise_dtypes=True))
            step.done(nc.gpsimd.iota(rowbase[:], [[SLOTS, B], [CAP, E]], base=0, channel_multiplier=0,
                                     allow_small_or_imprecise_dtypes=True))
            step.wait()
            step.then(nc.gpsimd.affine_select(out=ident[:], in_=ident[:], compare_op=ALU.is_equal, fill=0.0, base=0,
                                              pattern=[[-1, P]], channel_multiplier=1))
            step.then(nc.gpsimd.affine_select(out=before[:], in_=before[:], compare_op=ALU.is_gt, fill=0.0, base=0,
                                              pattern=[[1, P]], channel_multiplier=-1))
            for g in range(P // GROUP):
                r = slice(g * GROUP, (g + 1) * GROUP)
                step.then(nc.gpsimd.memset(m_quad[r, r], float(INNER) ** -0.5))
                if g < P // GROUP - 1:
                    step.then(nc.gpsimd.memset(m_lin[r, (g + 1) * GROUP:P], 1.0))
                step.then(nc.gpsimd.affine_select(out=m_quad[r, r], in_=m_quad[r, r], compare_op=ALU.is_ge, fill=0.0, base=0,
                                                  pattern=[[1, GROUP]], channel_multiplier=-1))
            for s, count in per_row.items():
                p.sem_inc(s, count)
            p.sem_inc(consts, 1)
            p.wait_ge(load_a, 112)
            for slots, i in [(d, i) for d in (xslots, yslots) for i in range(B * ST // T)]:
                nc.gpsimd.dma_start(slots[i * S:(i + 1) * S, :].rearrange("(t p) c -> p t c", p=P), xhat_r[:]).then_inc(zeroed, 16)
            p.wait_ge(zeroed, ZEROED)
            for k in ITER_A:
                scatter(p, k + 1)
            begin = step.n
            with p.Fori(2, B) as b:
                step.n = begin + b - 2
                gather(p, step, b - 1, b - 2)
                scatter(p, b + 1)
            with p.Fori(0, B) as b:
                step.n = begin + B - 2 + b
                gather(p, step, B + b - 1, (b + 2) % B)
                scatter(p, B + b + 1)
            step.n = begin + 2 * B - 2
            gather(p, step, 2 * B - 1, B - 2)
            gather(p, step, 2 * B, B - 1)

        @block.scalar
        def _(a):
            a.wait_ge(consts, 1)
            a.wait_ge(load_a, 112)
            for k in ITER_A:
                a_scalar(a, k + 1, 2 * k + 1)
                route_scalar(a, k + 1, 2 * k + 2)
                if k == 1:
                    a.wait_ge(load_f, 96)
                    experts_scalar(a, k)
            with a.Fori(2, B) as b:
                a_scalar(a, b + 1, 2 * b + 1)
                route_scalar(a, b + 1, 2 * b + 2)
                experts_scalar(a, b)
            with a.Fori(0, B) as b:
                c_scalar(a, b + 1, 2 * (B + b) + 1)
                route_scalar(a, B + b + 1, 2 * (B + b) + 2)
                experts_scalar(a, B + b)
            experts_scalar(a, 2 * B)

        @block.vector
        def _(v):
            v.wait_ge(consts, 1)
            v.wait_ge(load_x0, 16)
            v.wait_ge(load_a, 112)
            step = Steps(v, dve_step)
            for k in ITER_A:
                a_vector(v, step, k + 1, 2 * k + 1, k)
                if k == 0:
                    v.wait_ge(load_x, 16)
                    v.wait_ge(zeroed, ZEROED)
                route_vector(v, step, k + 1, 2 * k + 2, k)
            begin, per = step.n, 2 * LN_STEPS + 3 + ROUTE_STEPS + 1
            with v.Fori(2, B) as b:
                step.n = begin + (b - 2) * per
                a_vector(v, step, b + 1, 2 * b + 1, b)
                route_vector(v, step, b + 1, 2 * b + 2, b)
                combine_vector(v, step, b - 1, b - 2)
            step.n = begin + (B - 2) * per
            v.wait_ge(load_c, 64)
            step.done(nc.vector.tensor_scalar(wall[:, :, WQ:WQ + P], wall[:, :, WQ:WQ + P], HD ** -0.5, None, ALU.mult))
            nc.vector.tensor_scalar(wall[:, :, BQ:BQ + 1], wall[:, :, BQ:BQ + 1], HD ** -0.5, None, ALU.mult).then_inc(scaled, 1)
            begin, per = step.n, 2 * LN_STEPS + 1 + PAIRS * T + ROUTE_STEPS + 1
            with v.Fori(0, B) as b:
                step.n = begin + b * per
                c_vector(v, step, b + 1, 2 * (B + b) + 1, b)
                route_vector(v, step, B + b + 1, 2 * (B + b) + 2, b)
                combine_vector(v, step, B + b - 1, (b + 2) % B)
            step.n = begin + B * per
            combine_vector(v, step, 2 * B - 1, B - 2)
            combine_vector(v, step, 2 * B, B - 1)

        @block.tensor
        def _(pe):
            pe.wait_ge(consts, 1)
            pe.wait_ge(load_a, 112)
            for k in ITER_A:
                a_tensor(pe, k + 1, 2 * k + 1)
                if k == 0:
                    pe.wait_ge(load_f, 96)
                behind_tensor(pe, k + 1, 2 * k + 2, k > 0)
            with pe.Fori(2, B) as b:
                a_tensor(pe, b + 1, 2 * b + 1)
                behind_tensor(pe, b + 1, 2 * b + 2, True)
            with pe.Fori(0, B) as b:
                c_tensor(pe, b + 1, 2 * (B + b) + 1)
                behind_tensor(pe, B + b + 1, 2 * (B + b) + 2, True)
            experts_tensor(pe, 2 * B, lambda: None)


ZEROED = 2 * 16 * (B * ST // T)



def kernel(**inputs):
    import numpy as np
    import concourse.bacc as bacc
    from concourse.bass_utils import run_bass_kernel_spmd

    def get(name):
        return np.asarray(inputs["L0_" + name])

    def attn(name):
        return get("attn_a_" + name)

    cols_a = np.stack([*attn("bg").reshape(EH, P), attn("bin_")] +
                      [attn(n) for n in ("g_qq", "b_qq", "g_qk", "b_qk", "g_lq", "b_lq", "g_lk", "b_lk")], axis=1)
    wqkv = np.stack([get(f"attn_b_{c}_w").reshape(PAIRS, P, P).transpose(2, 0, 1) for c in "qkv"], axis=2).reshape(P, PAIRS, 3 * P)
    bqk = np.stack([get(f"attn_b_{c}_b").reshape(PAIRS, P).T for c in "qk"], axis=2)
    arrays = {
        "x": attn("x").reshape(B * S, P), "wv": attn("Wv"), "bv": attn("bv"), "wg": attn("Wg"), "win": attn("Win"),
        "wout": attn("Wout"), "bout": attn("bout"), "cols_a": cols_a, "wr": get("ffn_Wr"), "w1": get("ffn_W1"),
        "b1": get("ffn_b1").reshape(E * HC, P).T, "w2": get("ffn_W2"), "b2": get("ffn_b2").T,
        "wqkv": wqkv, "bqk": bqk, "bvv": get("attn_b_v_b").reshape(PAIRS, P),
        "wl": get("attn_b_l_w").T.reshape(PAIRS, P, P).transpose(1, 0, 2), "bl": get("attn_b_l_b").reshape(P),
    }
    arrays = {n: np.ascontiguousarray(a) for n, a in arrays.items()}
    nc = bacc.Bacc("TRN2", target_bir_lowering=False, num_devices=1)
    args = {n: nc.dram_tensor("in_" + n, a.shape, mybir.dt.from_np(a.dtype), kind="ExternalInput").ap() for n, a in arrays.items()}
    result = nc.dram_tensor("out_x", (B * S, P), F32, kind="ExternalOutput").ap()
    bass_hybrid(nc, **args, out=result)
    r = run_bass_kernel_spmd(nc, [{"in_" + n: a for n, a in arrays.items()}], core_ids=[0])
    return r.results[0]["out_x"].reshape(B, S, P)
```

```python
from contextlib import ExitStack

import concourse.bass as bass
from concourse import mybir

F32 = mybir.dt.float32
F32R = mybir.dt.float32r
BF16 = mybir.dt.bfloat16
U32 = mybir.dt.uint32
I32 = mybir.dt.int32
ALU = mybir.AluOpType
ACT = mybir.ActivationFunctionType
X_AXIS = mybir.AxisListType.X

P = 128
B = 4
S = 1024
T = S // P
HALF = 512
GROUP = 32
INNER = 256
EH = INNER // P
E = 8
CAP = int(S / E * 1.25)
HID = 512
HC = HID // P
SLOTS = E * CAP
ST = SLOTS // P
HEADS = 16
HD = 64
PAIRS = HEADS // 2
EPS = 1e-5
NEWTON = 3
SKIPPED = float(4 * B * SLOTS)
WQ, WK, LO, WV, BQ, BK, BV, WCOLS = 0, P, 2 * P, 4 * P, 5 * P, 5 * P + 1, 5 * P + 2, 6 * P + 2


def bass_hybrid(nc, x, wv, bv, wg, win, wout, bout, cols_a, wr, w1, b1, w2, b2, wqkv, bqk, bvv, wl, bl, out):
    with ExitStack() as keep:
        def sb(name, shape, dt=F32, stack=keep):
            return stack.enter_context(nc.sbuf_tensor(name, shape, dt))

        def sem(name):
            return keep.enter_context(nc.semaphore(name))

        bank = keep.enter_context(nc.psum_tensor("bank", [P, 8, HALF], F32))
        xres = sb("xres", [P, B * T, P])
        xhat = sb("xhat", [P, T, P])
        xhat_r = sb("xhat_r", [P, T, P])
        xT = sb("xT", [P, S])
        xT_hi = sb("xT_hi", [P, S], F32R)
        xT_lo = sb("xT_lo", [P, S], F32R)
        xT_r = sb("xT_r", [P, S])
        ident = sb("ident", [P, P])
        stats = sb("stats", [P, 2 * T, 6])
        meanvar = sb("meanvar", [P, 2 * T, 2])
        rstd = sb("rstd", [P, 2 * T])
        half_var = sb("half_var", [P, 2 * T])
        varp = sb("varp", [P, 2 * T])
        newton = sb("newton", [P, 2 * T])
        magic = sb("magic", [P, 2 * T], I32)
        w1_sb = sb("w1_sb", [P, E, HID])
        w2_sb = sb("w2_sb", [P, E, HC, P])
        b1_sb = sb("b1_sb", [P, E * HC])
        b2_sb = sb("b2_sb", [P, E])
        wr_sb = sb("wr_sb", [P, E])
        before = sb("before", [P, P], BF16)
        ones = sb("ones", [P, P], BF16)
        rev = sb("rev", [P, E])
        rowbase = sb("rowbase", [P, B, E])
        bl_sb = sb("bl_sb", [P, P])
        bout_sb = sb("bout_sb", [P, P])
        wl_sb = sb("wl_sb", [P, PAIRS, P])
        xslots = nc.dram_tensor("xslots", [B * SLOTS, P], F32, kind="Internal").ap()
        wpairs = nc.dram_tensor("wpairs", [PAIRS * P, WCOLS], F32, kind="Internal").ap()
        yslots = nc.dram_tensor("yslots", [B * SLOTS, P], F32, kind="Internal").ap()

        load_x0 = sem("load_x0")
        load_x = sem("load_x")
        load_a = sem("load_a")
        load_f = sem("load_f")
        load_w = [sem("load_w0"), sem("load_w1")]
        a_split = sem("a_split")
        w_split = sem("w_split")
        w_stored = sem("w_stored")
        consts = sem("consts")
        magic_set = sem("magic_set")
        pool_step = sem("pool_step")
        dve_step = sem("dve_step")
        zeroed = sem("zeroed")
        ln_xhat = sem("ln_xhat")
        ln_tr = sem("ln_tr")
        ln_xT = sem("ln_xT")
        ln_hi = sem("ln_hi")
        ln_lo = sem("ln_lo")
        a_xproj, a_gproj, a_vproj, a_lktr = sem("a_xproj"), sem("a_gproj"), sem("a_vproj"), sem("a_lktr")
        a_sq, a_sl, a_kv, a_o, a_out = sem("a_sq"), sem("a_sl"), sem("a_kv"), sem("a_o"), sem("a_out")
        a_xs, a_gs, a_v, a_lkt, a_usq = sem("a_xs"), sem("a_gs"), sem("a_v"), sem("a_lkt"), sem("a_usq")
        a_feat, a_vbias, a_u, a_at = sem("a_feat"), sem("a_vbias"), sem("a_u"), sem("a_at")
        a_state, a_gated, a_res = sem("a_state"), sem("a_gated"), sem("a_res")
        f_lg, f_pos, f_str, f_h, f_y, f_ytr = (sem(n) for n in ("f_lg", "f_pos", "f_str", "f_h", "f_y", "f_ytr"))
        f_sub, f_exp, f_m, f_idx = sem("f_sub"), sem("f_exp"), sem("f_m"), sem("f_idx")
        f_xs, f_ha, f_ya, f_ys = (sem(n) for n in ("f_xs", "f_ha", "f_ya", "f_ys"))
        f_sc, f_ld, f_st, f_comb = (sem(n) for n in ("f_sc", "f_ld", "f_st", "f_comb"))
        f_ga = [sem("f_ga0"), sem("f_ga1")]
        c_stage = [sem("c_stage0"), sem("c_stage1")]
        c_dup = [sem("c_dup0"), sem("c_dup1")]
        c_proj, c_hi, c_pev = (sem(n) for n in ("c_proj", "c_hi", "c_pev"))
        c_qk, c_max, c_exp, c_vs, c_av = (sem(n) for n in ("c_qk", "c_max", "c_exp", "c_vs", "c_av"))
        c_ctx, c_out, c_res = sem("c_ctx"), sem("c_out"), sem("c_res")
        stored = sem("stored")
        waits = sem("waits")

        def hold(engine, s, value):
            engine.wait_ge(s, value)
            engine.sem_inc(waits, 1)

        class Steps:
            def __init__(self, engine, s):
                self.engine, self.sem, self.n = engine, s, 0

            def wait(self):
                self.engine.wait_ge(self.sem, self.n)

            def done(self, ins):
                self.n = self.n + 1
                ins.then_inc(self.sem, 1)

            def then(self, ins):
                self.done(ins)
                self.wait()

        per_row = {
            ln_xhat: T, ln_tr: T, ln_xT: 2, ln_hi: 2, ln_lo: 2,
            a_xproj: 2, a_gproj: 4, a_vproj: T, a_lktr: T, a_sq: T, a_sl: T, a_kv: T - 1, a_o: 2 * T, a_out: T,
            a_xs: 2, a_gs: 4, a_v: 4, a_lkt: 2, a_usq: 2, a_feat: 4, a_vbias: 4, a_u: 2, a_at: 2, a_state: T - 1,
            a_gated: 4, a_res: 2,
            f_lg: 1, f_pos: 1, f_str: ST, f_h: 2 * E, f_y: E, f_ytr: ST, f_sub: 1, f_exp: 1, f_m: 1, f_idx: 1,
            f_xs: 3, f_ha: E, f_ya: E, f_ys: 3, f_ld: 16, f_st: 16, f_comb: 2 * T,
            c_stage[0]: 8 * PAIRS, c_stage[1]: 8 * PAIRS, c_proj: 6 * PAIRS, c_hi: 8 * PAIRS, c_pev: 6 * PAIRS, c_dup[0]: 32 * PAIRS, c_dup[1]: 32 * PAIRS,
            c_qk: 2 * T * PAIRS, c_max: 2 * T * PAIRS, c_exp: 2 * T * PAIRS, c_vs: T * PAIRS, c_av: T * PAIRS,
            c_ctx: 2 * PAIRS, c_out: 2 * PAIRS, c_res: 2 * PAIRS,
        }

        LN_ROUTE, LN_MAIN = 0, 5
        def norms_vector(v, step, norms, m=None):
            def row_tile(b, t):
                return xres[:, bass.ds(b * T + t, 1), :].rearrange("p a c -> p (a c)")
            w = len(norms) * T
            for i, (n, b, xh) in enumerate(norms):
                for t in range(T):
                    step.done(nc.vector.bn_stats(stats[:, i * T + t, :], row_tile(b, t)))
            hold(v, dve_step, step.n)
            for t in range(w):
                ins = nc.vector.bn_aggr(meanvar[:, t, :], stats[:, t, :])
            step.then(ins)
            y, z = rstd[:, 0:w], newton[:, 0:w]
            step.then(nc.vector.tensor_scalar(varp[:, 0:w], meanvar[:, 0:w, 1], EPS, None, ALU.add))
            step.done(nc.vector.tensor_scalar(half_var[:, 0:w], varp[:, 0:w], -0.5, None, ALU.mult))
            step.then(nc.vector.tensor_scalar(z.bitcast(I32), varp[:, 0:w].bitcast(I32), 1, None, ALU.arith_shift_right))
            step.then(nc.vector.tensor_tensor(y.bitcast(I32), magic[:, 0:w], z.bitcast(I32), ALU.subtract))
            for _ in range(NEWTON):
                step.then(nc.vector.tensor_tensor(z, y, y, ALU.mult))
                step.then(nc.vector.tensor_tensor(z, z, half_var[:, 0:w], ALU.mult))
                step.then(nc.vector.scalar_tensor_tensor(out=y, in0=z, scalar=1.5, in1=y, op0=ALU.add, op1=ALU.mult))
            if m is not None:
                hold(v, f_ld, 16 * m)
            for i, (n, b, xh) in enumerate(norms):
                if not (isinstance(n, int) and n == 1):
                    v.wait_ge(ln_tr, (n - 1) * T)
                for t in range(T):
                    c = i * T + t
                    nc.vector.tensor_scalar(xh[:, t, :], row_tile(b, t), meanvar[:, c, 0:1], rstd[:, c:c + 1],
                                            ALU.subtract, ALU.mult).then_inc(ln_xhat, 1)

        def bias_vector(v, step, n, b, bias):
            xb = xres[:, bass.ds(b * T, T), :]
            v.wait_ge(ln_xhat, (n + 1) * T)
            step.done(nc.vector.tensor_tensor(xb, xb, bias[:].unsqueeze(1).to_broadcast([P, T, P]), ALU.add))

        def xT_scalar(a, n):
            for h in range(2):
                c = slice(h * HALF, (h + 1) * HALF)
                a.wait_ge(ln_tr, n * T + 4 * (h + 1))
                nc.scalar.activation(xT[:, c], bank[:, LN_MAIN + h, :], ACT.Copy).then_inc(ln_xT, 1)
                a.wait_ge(ln_xT, 2 * n + h + 1)
                nc.scalar.activation(xT_hi[:, c], xT[:, c], ACT.Copy).then_inc(ln_hi, 1)

        def xT_lo_vector(v, n):
            for h in range(2):
                c = slice(h * HALF, (h + 1) * HALF)
                v.wait_ge(ln_hi, n + h + 2)
                nc.vector.tensor_tensor(xT_lo[:, c], xT[:, c], xT_hi[:, c].bitcast(F32), ALU.subtract).then_inc(ln_lo, 1)

        def ln_tensor(pe, n, xh, bk):
            for t in range(T):
                pe.wait_ge(ln_xhat, n * T + t + 1)
                nc.tensor.transpose(bank[:, bk + t // 4, (t % 4) * P:(t % 4 + 1) * P], xh[:, t, :], ident[:]).then_inc(ln_tr, 1)

        def ln_scalar(a, n, dst, bk):
            for h in range(2):
                a.wait_ge(ln_tr, n * T + 4 * (h + 1))
                nc.scalar.activation(dst[:, h * HALF:(h + 1) * HALF], bank[:, bk + h, :], ACT.Copy).then_inc(ln_xT, 1)

        def cols(i, n=P):
            return slice(i * n, (i + 1) * n)

        stage_f = keep
        def small(name, dt=F32):
            return sb(name, [P, T, E], dt, stack=stage_f)
        lg, ex, pr, eq, key, pr2, tmp = (small(n) for n in ("lg", "ex", "pr", "eq", "key", "pr2", "tmp"))
        oh, oh_row, oh_kept = (sb(n, [P, 2, T, E], stack=stage_f) for n in ("oh", "oh_row", "oh_kept"))
        chosen = small("chosen", BF16)
        rowmat, keepmat = small("rowmat"), small("keepmat")
        nmax, rsum, rinv, rk = (sb(n, [P, T], stack=stage_f) for n in ("nmax", "rsum", "rinv", "rk"))
        ptop = sb("ptop", [P, 2, T], stack=stage_f)
        kept = sb("kept", [P, 2, T], stack=stage_f)
        wtok = sb("wtok", [P, 2, T], stack=stage_f)
        wtok_ring = sb("wtok_ring", [P, B, 2 * T], stack=stage_f)
        rowf = sb("rowf", [P, 2, T], stack=stage_f)
        skip = sb("skip", [P, 2, T], stack=stage_f)
        row_g = sb("row_g", [P, 2, T], U32, stack=stage_f)
        row_ring = sb("row_ring", [P, B, 2 * T], U32, stack=stage_f)
        row_s = sb("row_s", [P, 2, T], U32, stack=stage_f)
        slots_sb = sb("slots_sb", [P, ST, P], stack=stage_f)
        xsT = sb("xsT", [P, SLOTS], stack=stage_f)
        hT = sb("hT", [P, 2, HC, CAP], stack=stage_f)
        yT = sb("yT", [P, SLOTS], stack=stage_f)
        yg = sb("yg", [P, 2, T, P], stack=stage_f)
        THIRD_A, THIRD_C = 4, 1
        TR = [(2, 0, 4), (3, 4, 8), (4, 8, ST)]

        def over_e(t):
            return t.unsqueeze(2).to_broadcast([P, T, E])

        def logits_tensor(pe, m, n):
            pe.wait_ge(ln_xT, 2 * n + 2)
            for t in range(T):
                ins = nc.tensor.matmul(bank[:, 0, t * E:(t + 1) * E], xT_r[:, cols(t)], wr_sb[:], start=True, stop=True)
            ins.then_inc(f_lg, 1)

        def positions(pe, m):
            pe.wait_ge(f_m, m + 1)
            pos = bank[:, 1, 0:T * E].rearrange("p (t e) -> p t e", e=E)
            nc.tensor.matmul(bank[:, 1, 0:T * E], before[:], chosen[:].rearrange("p t e -> p (t e)"), start=True, stop=False)
            for t in range(T - 1):
                ins = nc.tensor.matmul(pos[:, t + 1:T, :], ones[:], chosen[:, t:t + 1, :].to_broadcast([P, T - 1 - t, E]),
                                       start=False, stop=(t == T - 2))
            ins.then_inc(f_pos, 1)

        def slots_tensor(pe, m, third):
            pe.wait_ge(f_ld, 16 * (m + 1))
            for bk, lo, hi in TR[:2] + [(third, *TR[2][1:])]:
                for i in range(lo, hi):
                    nc.tensor.transpose(bank[:, bk, cols(i - lo)], slots_sb[:, i, :], ident[:]).then_inc(f_str, 1)

        def experts_tensor(pe, m, beside, residual=None):
            def up(e):
                if e >= 2:
                    pe.wait_ge(f_ha, E * m + e - 1)
                for c in range(HC):
                    ins = nc.tensor.matmul(bank[:, 2 + 2 * (e % 2) + c // 2, cols(c % 2, CAP)], w1_sb[:, e, cols(c)],
                                           xsT[:, cols(e, CAP)], start=True, stop=True)
                    if c % 2:
                        ins.then_inc(f_h, 1)

            def down(e):
                if e == 0 and residual:
                    pe.wait_ge(*residual)
                pe.wait_ge(f_ha, E * m + e + 1)
                if e >= 2:
                    pe.wait_ge(f_ya, E * m + e - 1)
                for c in range(HC):
                    ins = nc.tensor.matmul(bank[:, 6 + e % 2, 0:CAP], w2_sb[:, e, c, :], hT[:, e % 2, c, :],
                                           start=(c == 0), stop=(c == HC - 1))
                ins.then_inc(f_y, 1)

            pe.wait_ge(f_xs, 3 * m + 2)
            up(0)
            for e in range(1, E):
                if e == 1:
                    pe.wait_ge(f_xs, 3 * (m + 1))
                up(e)
                down(e - 1)
                beside(e)
            down(E - 1)
            beside(E)
            pe.wait_ge(f_ya, E * (m + 1))
            for bk, lo, hi in TR:
                for i in range(lo, hi):
                    nc.tensor.transpose(bank[:, bk, cols(i - lo)], yT[:, cols(i)], ident[:]).then_inc(f_ytr, 1)

        def behind_tensor(pe, m, n, residual, with_experts=True):
            def beside(e):
                if e == 4:
                    ln_tensor(pe, n, xhat_r, LN_ROUTE)
                if e == 5:
                    logits_tensor(pe, m, n)
                if e == E:
                    positions(pe, m)
                    pe.wait_ge(f_ya, E * m - 1)
                    ln_tensor(pe, n + 1, xhat, LN_MAIN)
            if with_experts:
                experts_tensor(pe, m - 1, beside, residual)
            else:
                pe.wait_ge(*residual)
                for e in (4, 5, E):
                    beside(e)

        def last_behind_tensor(pe, m, n, residual):
            def beside(e):
                if e == 1:
                    positions(pe, m)
            pe.wait_ge(f_xs, 3 * m)
            ln_tensor(pe, n, xhat_r, LN_ROUTE)
            logits_tensor(pe, m, n)
            experts_tensor(pe, m - 1, beside, residual)

        def probs_scalar(a, m):
            a.wait_ge(f_sub, m + 1)
            nc.scalar.activation(ex[:], lg[:], ACT.Exp).then_inc(f_exp, 1)

        def behind_scalar(a, m, n, third, with_experts=True):
            def beside(e):
                if e == 4:
                    ln_scalar(a, n, xT_r, LN_ROUTE)
                if e == 5:
                    probs_scalar(a, m)
                if e == E:
                    xT_scalar(a, n + 1)
            if with_experts:
                slots_scalar(a, m - 1, third)
                experts_scalar(a, m - 1, beside)
            else:
                for e in (4, 5, E):
                    beside(e)

        def last_behind_scalar(a, m, n):
            slots_scalar(a, m - 1, THIRD_C)
            ln_scalar(a, n, xT_r, LN_ROUTE)
            probs_scalar(a, m)
            experts_scalar(a, m - 1, lambda e: None)

        def slots_scalar(a, m, third):
            for bk, lo, hi in TR[:2] + [(third, *TR[2][1:])]:
                a.wait_ge(f_str, ST * m + hi)
                nc.scalar.activation(xsT[:, lo * P:hi * P], bank[:, bk, 0:(hi - lo) * P], ACT.Copy).then_inc(f_xs, 1)

        def experts_scalar(a, m, beside):
            def hidden(e):
                if e >= 2:
                    a.wait_ge(f_y, E * m + e - 1)
                for c in range(HC):
                    if c % 2 == 0:
                        a.wait_ge(f_h, 2 * E * m + 2 * e + c // 2 + 1)
                    ins = nc.scalar.activation(hT[:, e % 2, c, :], bank[:, 2 + 2 * (e % 2) + c // 2, cols(c % 2, CAP)],
                                               ACT.Relu, bias=b1_sb[:, e * HC + c:e * HC + c + 1])
                ins.then_inc(f_ha, 1)

            def answer(e):
                a.wait_ge(f_y, E * m + e + 1)
                nc.scalar.activation(yT[:, cols(e, CAP)], bank[:, 6 + e % 2, 0:CAP], ACT.Identity,
                                     bias=b2_sb[:, e:e + 1]).then_inc(f_ya, 1)

            hidden(0)
            for e in range(1, E):
                hidden(e)
                answer(e - 1)
                beside(e)
            answer(E - 1)
            beside(E)
            for bk, lo, hi in TR:
                a.wait_ge(f_ytr, ST * m + hi)
                nc.scalar.activation(slots_sb[:, lo:hi, :], bank[:, bk, 0:(hi - lo) * P].rearrange("p (t c) -> p t c", c=P),
                                     ACT.Copy).then_inc(f_ys, 1)

        def route_vector(v, step, m, b):
            v.wait_ge(f_lg, m + 1)
            logits = bank[:, 0, 0:T * E].rearrange("p (t e) -> p t e", e=E)
            step.then(nc.vector.tensor_reduce(nmax[:], logits, X_AXIS, ALU.max))
            nc.vector.tensor_tensor(lg[:], logits, over_e(nmax[:]), ALU.subtract).then_inc(f_sub, 1)
            v.wait_ge(f_exp, m + 1)
            step.then(nc.vector.tensor_reduce(rsum[:], ex[:], X_AXIS, ALU.add))
            step.then(nc.vector.reciprocal(rinv[:], rsum[:]))
            step.then(nc.vector.tensor_tensor(pr[:], ex[:], over_e(rinv[:]), ALU.mult))
            p_now = pr
            for k in range(2):
                step.then(nc.vector.tensor_reduce(ptop[:, k, :], p_now[:], X_AXIS, ALU.max))
                step.then(nc.vector.tensor_tensor(eq[:], p_now[:], over_e(ptop[:, k, :]), ALU.is_equal))
                step.then(nc.vector.tensor_tensor(key[:], eq[:], rev[:].unsqueeze(1).to_broadcast([P, T, E]), ALU.mult))
                step.then(nc.vector.tensor_reduce(rk[:], key[:], X_AXIS, ALU.max))
                step.then(nc.vector.tensor_tensor(oh[:, k], key[:], over_e(rk[:]), ALU.is_equal))
                if k == 0:
                    step.then(nc.vector.scalar_tensor_tensor(out=pr2[:], in0=oh[:, 0], scalar=-2.0, in1=pr[:],
                                                             op0=ALU.mult, op1=ALU.add))
                    p_now = pr2
            nc.vector.tensor_tensor(chosen[:], oh[:, 0], oh[:, 1], ALU.add).then_inc(f_m, 1)
            v.wait_ge(f_pos, m + 1)
            pos = bank[:, 1, 0:T * E].rearrange("p (t e) -> p t e", e=E)
            step.done(nc.vector.tensor_scalar(keepmat[:], pos, float(CAP), None, ALU.is_lt))
            step.then(nc.vector.tensor_scalar(tmp[:], pos, float(CAP - 1), None, ALU.min))
            step.then(nc.vector.tensor_tensor(rowmat[:], tmp[:],
                                              rowbase[:, bass.ds(b, 1), :].to_broadcast([P, T, E]), ALU.add))
            step.done(nc.vector.tensor_tensor(oh_row[:], oh[:], rowmat[:].unsqueeze(1).to_broadcast([P, 2, T, E]), ALU.mult))
            step.then(nc.vector.tensor_tensor(oh_kept[:], oh[:], keepmat[:].unsqueeze(1).to_broadcast([P, 2, T, E]), ALU.mult))
            step.done(nc.vector.tensor_reduce(rowf[:], oh_row[:], X_AXIS, ALU.add))
            step.then(nc.vector.tensor_reduce(kept[:], oh_kept[:], X_AXIS, ALU.add))
            step.done(nc.vector.tensor_copy(row_ring[:, bass.ds(b, 1), :].rearrange("p a c -> p (a c)"),
                                            rowf[:].rearrange("p k t -> p (k t)")))
            step.then(nc.vector.tensor_scalar(skip[:], kept[:], -SKIPPED, SKIPPED, ALU.mult, ALU.add))
            step.done(nc.vector.tensor_tensor(wtok_ring[:, bass.ds(b, 1), :].rearrange("p a c -> p (a c)"),
                                              ptop[:].rearrange("p k t -> p (k t)"), kept[:].rearrange("p k t -> p (k t)"), ALU.mult))
            nc.vector.tensor_tensor(row_s[:], rowf[:], skip[:], ALU.add).then_inc(f_idx, 1)

        ROUTE_STEPS = 4 + 5 + 1 + 5 + 3 + 4 + 3

        def norm_steps(rows):
            return rows * T + 5 + 3 * NEWTON

        def combine_tiles(v, step, m, b, k, tiles):
            if k == 0 and tiles[0] == 0:
                step.then(nc.vector.tensor_copy(wtok[:].rearrange("p k t -> p (k t)"),
                                                wtok_ring[:, bass.ds(b, 1), :].rearrange("p a c -> p (a c)")))
            if tiles[0] == 0:
                hold(v, f_ga[k], 16 * T * m)
            if k == 1 and tiles[0] == 0:
                hold(v, f_comb, 2 * T * m + T)
            for t in tiles:
                xr = xres[:, bass.ds(b * T + t, 1), :].rearrange("p a c -> p (a c)")
                nc.vector.scalar_tensor_tensor(out=xr, in0=yg[:, k, t, :], scalar=wtok[:, k, t:t + 1], in1=xr,
                                               op0=ALU.mult, op1=ALU.add).then_inc(f_comb, 1)

        def combine_vector(v, step, m, b):
            for k in range(2):
                combine_tiles(v, step, m, b, k, range(T))
            hold(v, f_comb, 2 * T * (m + 1))

        def scatter(p, m):
            hold(p, f_idx, m + 1)
            for k in range(2):
                for t in range(T):
                    nc.gpsimd.indirect_dma_start(out=xslots[:, :], out_offset=bass.IndirectOffsetOnAxis(ap=row_s[:, k, t:t + 1], axis=0),
                                                 in_=xhat_r[:, t, :], in_offset=None,
                                                 bounds_check=B * SLOTS - 1, oob_is_err=False).then_inc(f_sc, 16)

        def gather(p, step, m, b):
            hold(p, f_comb, 2 * T * m)
            step.then(nc.gpsimd.tensor_copy(row_g[:].rearrange("p k t -> p (k t)"),
                                            row_ring[:, bass.ds(b, 1), :].rearrange("p a c -> p (a c)")))
            hold(p, f_st, 16 * (m + 1))
            for k in range(2):
                for t in range(T):
                    nc.gpsimd.indirect_dma_start(out=yg[:, k, t, :], out_offset=None, in_=yslots[:, :],
                                                 in_offset=bass.IndirectOffsetOnAxis(ap=row_g[:, k, t:t + 1], axis=0),
                                                 bounds_check=B * SLOTS - 1, oob_is_err=False).then_inc(f_ga[k], 16)

        def load_slots(sp, m, b):
            hold(sp, f_st, 16 * m)
            hold(sp, f_sc, 256 * m)
            sp.dma_start(slots_sb[:], xslots[bass.ds(b * SLOTS, SLOTS), :].rearrange("(i p) c -> p i c", p=P)).then_inc(f_ld, 16)

        def store_slots(sp, m, b):
            hold(sp, f_ys, 3 * (m + 1))
            sp.dma_start(yslots[bass.ds(b * SLOTS, SLOTS), :].rearrange("(i p) c -> p i c", p=P), slots_sb[:]).then_inc(f_st, 16)

        stage_a = ExitStack()
        wa_sb = sb("wa_sb", [P, P + 2 * INNER], stack=stage_a)
        wa_hi, wa_lo = (sb(n, [P, P + 2 * INNER], F32R, stack=stage_a) for n in ("wa_hi", "wa_lo"))
        WG, WVA = P, P + INNER
        w_raw = [sb(f"w_raw{i}", [P, LO], stack=stage_a) for i in range(2)]
        w_parts = [sb(f"w_parts{i}", [P, WCOLS], F32R, stack=stage_a) for i in range(2)]
        wout_sb = sb("wout_sb", [P, EH, P], stack=stage_a)
        bv_sb = sb("bv_sb", [P, INNER], stack=stage_a)
        ca = sb("ca", [P, 11], stack=stage_a)
        m_quad = sb("m_quad", [P, P], stack=stage_a)
        m_lin = sb("m_lin", [P, P], stack=stage_a)
        base = sb("base", [P, S], stack=stage_a)
        qqT, qkT, lqT, lkT = (sb(n, [P, S], stack=stage_a) for n in ("qqT", "qkT", "lqT", "lkT"))
        gateT = sb("gateT", [P, EH, S], stack=stage_a)
        vact = sb("vact", [P, T, INNER], stack=stage_a)
        lk = sb("lk", [P, T, P], stack=stage_a)
        relu_m = sb("relu_m", [P, S], stack=stage_a)
        attnT = sb("attnT", [P, S], stack=stage_a)
        state = sb("state", [P, T, INNER], stack=stage_a)
        V_BANK = [0, 1, 6, 7]
        KV_BANK = [6, 6, 7, 7, 4, 4, 5]

        def a_tensor(pe, r, n, with_experts=True):
            for h in range(2):
                pe.wait_ge(ln_hi, n + h + 2)
                x_hi, x_lo, o = xT_hi[:, cols(h, HALF)], xT_lo[:, cols(h, HALF)], bank[:, 7 - h, :]
                nc.tensor.matmul(o, wa_hi[:, 0:P], x_hi, start=True, stop=False)
                nc.tensor.matmul(o, wa_lo[:, 0:P], x_hi, start=False, stop=False)
                pe.wait_ge(ln_lo, n + h + 2)
                nc.tensor.matmul(o, wa_hi[:, 0:P], x_lo, start=False, stop=True).then_inc(a_xproj, 1)
            if not (isinstance(r, int) and r <= 2):
                pe.wait_ge(f_ys, 3 * (r - 1))
            for e in range(EH):
                c = slice(WG + e * P, WG + (e + 1) * P)
                for h in range(2):
                    x_hi, x_lo, o = xT_hi[:, cols(h, HALF)], xT_lo[:, cols(h, HALF)], bank[:, 4 - 2 * e + h, :]
                    nc.tensor.matmul(o, wa_hi[:, c], x_hi, start=True, stop=False)
                    nc.tensor.matmul(o, wa_lo[:, c], x_hi, start=False, stop=False)
                    nc.tensor.matmul(o, wa_hi[:, c], x_lo, start=False, stop=True).then_inc(a_gproj, 1)
            pe.wait_ge(f_idx, r)
            for t in range(T):
                if t == 4:
                    pe.wait_ge(a_xs, 2 * r + 2)
                x_hi, x_lo, o = xT_hi[:, cols(t)], xT_lo[:, cols(t)], bank[:, V_BANK[t // 2], cols(t % 2, INNER)]
                nc.tensor.matmul(o, x_hi, wa_hi[:, WVA:], start=True, stop=False)
                nc.tensor.matmul(o, x_hi, wa_lo[:, WVA:], start=False, stop=False)
                nc.tensor.matmul(o, x_lo, wa_hi[:, WVA:], start=False, stop=True).then_inc(a_vproj, 1)
            pe.wait_ge(a_gs, 4 * r + 2)
            pe.wait_ge(a_feat, 4 * r + 1)
            for t in range(T):
                nc.tensor.transpose(bank[:, 4 + t // 4, cols(t % 4)], lkT[:, cols(t)], ident[:]).then_inc(a_lktr, 1)
            pe.wait_ge(a_gs, 4 * r + 4)
            pe.wait_ge(a_feat, 4 * r + 3)
            for t in range(T):
                nc.tensor.matmul(bank[:, 2 + t // 4, cols(t % 4)], qkT[:, cols(t)], qqT[:, cols(t)],
                                 start=True, stop=True).then_inc(a_sq, 1)
            pe.wait_ge(a_feat, 4 * r + 4)
            pe.wait_ge(a_vbias, 4 * r + 2)
            for t in range(T):
                nc.tensor.matmul(bank[:, t // 4, cols(t % 4)], lkT[:, cols(t)], lqT[:, cols(t)],
                                 start=True, stop=True).then_inc(a_sl, 1)
            pe.wait_ge(a_v, 4 * r + 4)
            pe.wait_ge(a_lkt, 2 * r + 2)
            for t in range(T - 1):
                nc.tensor.matmul(bank[:, KV_BANK[t], cols(t % 2, INNER)], lk[:, t, :], vact[:, t, :],
                                 start=True, stop=True).then_inc(a_kv, 1)
            pe.wait_ge(a_at, 2 * r + 2)
            for e in range(EH):
                for t in range(T):
                    o = bank[:, (2 if e == 0 else 0) + t // 4, cols(t % 4)]
                    ins = nc.tensor.matmul(o, vact[:, t, cols(e)], attnT[:, cols(t)], start=True, stop=(t == 0))
                    if t > 0:
                        if e == 0:
                            pe.wait_ge(a_state, 7 * r + t)
                        ins = nc.tensor.matmul(o, state[:, t, cols(e)], lqT[:, cols(t)], start=False, stop=True)
                    ins.then_inc(a_o, 1)
            if with_experts:
                pe.wait_ge(a_state, 7 * (r + 1))
                pe.wait_ge(a_gated, 4 * r + 2)
                slots_tensor(pe, r - 1, THIRD_A)
            pe.wait_ge(a_gated, 4 * r + 4)
            for t in range(T):
                for e in range(EH):
                    ins = nc.tensor.matmul(bank[:, 6 + t // 4, cols(t % 4)], gateT[:, e, cols(t)], wout_sb[:, e, :],
                                           start=(e == 0), stop=(e == EH - 1))
                ins.then_inc(a_out, 1)

        def a_scalar(a, r):
            for h in range(2):
                a.wait_ge(a_xproj, 2 * r + h + 1)
                nc.scalar.activation(base[:, cols(h, HALF)], bank[:, 7 - h, :], ACT.Silu, bias=ca[:, 2:3]).then_inc(a_xs, 1)
            for e in range(EH):
                for h in range(2):
                    a.wait_ge(a_gproj, 4 * r + 2 * e + h + 1)
                    nc.scalar.activation(gateT[:, e, cols(h, HALF)], bank[:, 4 - 2 * e + h, :], ACT.Silu,
                                         bias=ca[:, e:e + 1]).then_inc(a_gs, 1)
            for k in range(4):
                a.wait_ge(a_vbias, 4 * r + k + 1)
                nc.scalar.activation(vact[:, 2 * k:2 * k + 2, :], vact[:, 2 * k:2 * k + 2, :], ACT.Silu).then_inc(a_v, 1)
            for h in range(2):
                a.wait_ge(a_lktr, T * r + 4 * (h + 1))
                nc.scalar.activation(lk[:, 4 * h:4 * h + 4, :], bank[:, 4 + h, :].rearrange("p (t c) -> p t c", c=P),
                                     ACT.Copy).then_inc(a_lkt, 1)
            for h in range(2):
                a.wait_ge(a_u, 2 * r + h + 1)
                nc.scalar.activation(relu_m[:, cols(h, HALF)], relu_m[:, cols(h, HALF)], ACT.Square).then_inc(a_usq, 1)

        def split_vector(v, step, b):
            for i in range(2):
                v.wait_ge(load_w[i], 64 * (b + 1))
                raw, hi, lo = w_raw[i][:, 0:LO], w_parts[i][:, 0:LO], w_parts[i][:, LO:2 * LO]
                bq = w_parts[i][:, BQ:BQ + 1].bitcast(F32)
                step.done(nc.vector.tensor_scalar(w_raw[i][:, WQ:WQ + P], w_raw[i][:, WQ:WQ + P], HD ** -0.5, None, ALU.mult))
                step.then(nc.vector.tensor_scalar(bq, bq, HD ** -0.5, None, ALU.mult))
                step.then(nc.vector.tensor_copy(hi, raw))
                nc.vector.tensor_tensor(lo, raw, hi.bitcast(F32), ALU.subtract).then_inc(w_split, 1)

        def split_loads(sp, b):
            for i in range(2):
                biases, pair = w_parts[i][:, BQ:].bitcast(F32), 2 * b + i
                sp.dma_start(w_raw[i][:], wqkv[:, pair, 0:LO]).then_inc(load_w[i], 16)
                sp.dma_start(w_parts[i][:, WV:WV + P].bitcast(F32), wqkv[:, pair, LO:]).then_inc(load_w[i], 16)
                sp.dma_start(biases[:, 0:2], bqk[:, pair, :]).then_inc(load_w[i], 16)
                sp.dma_start(biases[:, 2:], bvv[pair, :].partition_broadcast(P)).then_inc(load_w[i], 16)

        def split_stores(sp, b):
            for i in range(2):
                pair = 2 * b + i
                sp.wait_ge(w_split, pair + 1)
                sp.dma_start(wpairs[pair * P:(pair + 1) * P, :], w_parts[i][:].bitcast(F32)).then_inc(w_stored, 16)

        def a_vector(v, step, r, n, b):
            xT_lo_vector(v, n)
            bias_vector(v, step, n, b, bout_sb)
            split_vector(v, step, b)
            v.wait_ge(a_xs, 2 * r + 2)
            for dst, c in ((lkT, 9), (qkT, 5), (qqT, 3), (lqT, 7)):
                nc.vector.tensor_scalar(dst[:], base[:], ca[:, c:c + 1], ca[:, c + 1:c + 2], ALU.mult, ALU.add).then_inc(a_feat, 1)
            for k in range(4):
                v.wait_ge(a_vproj, T * r + 2 * (k + 1))
                nc.vector.tensor_tensor(vact[:, 2 * k:2 * k + 2, :], bank[:, V_BANK[k], :].rearrange("p (t c) -> p t c", c=INNER),
                                        bv_sb[:].unsqueeze(1).to_broadcast([P, 2, INNER]), ALU.add).then_inc(a_vbias, 1)
            for h in range(2):
                v.wait_ge(a_sq, T * r + 4 * (h + 1))
                nc.vector.scalar_tensor_tensor(
                    out=relu_m[:, cols(h, HALF)].rearrange("p (t c) -> p t c", c=P),
                    in0=bank[:, 2 + h, :].rearrange("p (t c) -> p t c", c=P), scalar=0.0,
                    in1=m_quad[:].unsqueeze(1).to_broadcast([P, 4, P]), op0=ALU.max, op1=ALU.mult).then_inc(a_u, 1)
            for h in range(2):
                v.wait_ge(a_sl, T * r + 4 * (h + 1))
                step.done(nc.vector.tensor_tensor(
                    attnT[:, cols(h, HALF)].rearrange("p (t c) -> p t c", c=P),
                    bank[:, h, :].rearrange("p (t c) -> p t c", c=P),
                    m_lin[:].unsqueeze(1).to_broadcast([P, 4, P]), ALU.mult))
            step.wait()
            for h in range(2):
                v.wait_ge(a_usq, 2 * r + h + 1)
                nc.vector.tensor_tensor(attnT[:, cols(h, HALF)], relu_m[:, cols(h, HALF)], attnT[:, cols(h, HALF)],
                                        ALU.add).then_inc(a_at, 1)
            for t in range(1, T):
                v.wait_ge(a_kv, 7 * r + min(t + t % 2, T - 1))
                kv = bank[:, KV_BANK[t - 1], cols((t - 1) % 2, INNER)]
                if t == 1:
                    nc.vector.tensor_copy(state[:, t, :], kv).then_inc(a_state, 1)
                else:
                    v.wait_ge(a_state, 7 * r + t - 1)
                    nc.vector.tensor_tensor(state[:, t, :], kv, state[:, t - 1, :], ALU.add).then_inc(a_state, 1)
            for e in range(EH):
                for h in range(2):
                    v.wait_ge(a_o, 2 * T * r + T * e + 4 * (h + 1))
                    nc.vector.tensor_tensor(gateT[:, e, cols(h, HALF)], bank[:, (2 if e == 0 else 0) + h, :],
                                            gateT[:, e, cols(h, HALF)], ALU.mult).then_inc(a_gated, 1)
            for h in range(2):
                v.wait_ge(a_out, T * r + 4 * (h + 1))
                xr = xres[:, bass.ds(b * T + 4 * h, 4), :]
                nc.vector.tensor_tensor(xr, bank[:, 6 + h, :].rearrange("p (t c) -> p t c", c=P), xr, ALU.add).then_inc(a_res, 1)
            hold(v, a_res, 2 * r + 2)
        stage_a.close()

        stage_c = ExitStack()
        ws = [sb(f"ws{i}", [P, WCOLS], F32R, stack=stage_c) for i in range(2)]
        qst = [[sb(f"q{i}{h}", [P, 2, S], F32R, stack=stage_c) for h in range(2)] for i in range(2)]
        kst = [[sb(f"k{i}{h}", [P, S], F32R, stack=stage_c) for h in range(2)] for i in range(2)]
        vst = [sb(f"v{i}", [P, T, P], stack=stage_c) for i in range(2)]
        prob = [[sb(f"prob{i}{h}", [P, S], stack=stage_c) for h in range(2)] for i in range(2)]
        vsc = [sb(f"vsc{i}", [P, P], stack=stage_c) for i in range(2)]
        nmx = sb("nmx", [P, 4], stack=stage_c)
        zsum = sb("zsum", [P, 4], stack=stage_c)
        zinv = sb("zinv", [P, 4], stack=stage_c)
        ctxT = sb("ctxT", [P, S], stack=stage_c)
        SC = [(0, 1), (2, 3)]
        CX = (4, 5)
        PJ = (6, 7)
        FIRST_PJ = (7, 6, 5, 2, 4, 5)
        SPAN = 2 * T

        def rows(h):
            return slice(h * HD, (h + 1) * HD)

        def project(pe, par, pi, k, bk, n=None):
            w = ws[par]
            if k == 0:
                pe.wait_ge(c_stage[par], 8 * (pi - par + 2))
            if n is not None and k == 1:
                pe.wait_ge(ln_hi, n + 3)
            if k < 4:
                c, x_hi, x_lo = WQ if k < 2 else WK, xT_hi[:, cols(k % 2, HALF)], xT_lo[:, cols(k % 2, HALF)]
                nc.tensor.matmul(bank[:, bk, :], w[:, c:c + P], x_hi, start=True, stop=False)
                nc.tensor.matmul(bank[:, bk, :], w[:, LO + c:LO + c + P], x_hi, start=False, stop=False)
                if n is not None and k < 2:
                    pe.wait_ge(ln_lo, n + k + 2)
                ins = nc.tensor.matmul(bank[:, bk, :], w[:, c:c + P], x_lo, start=False, stop=True)
            else:
                for t in range(4):
                    ins = nc.tensor.matmul(bank[:, bk, cols(t)], xT[:, cols(4 * (k - 4) + t)], w[:, WV:WV + P].bitcast(F32),
                                           start=True, stop=True)
            ins.then_inc(c_proj, 1)

        def out_tensor(pe, pi, pair_row, n, last):
            if n == 0:
                pe.wait_ge(c_ctx, 2 * (pi + 1))
            if last:
                pe.wait_ge(c_res, 2 * pi - 1 + n)
            else:
                pe.wait_ge(c_pev, 6 * (pi + 3) - 1 + n)
            for t in range(4):
                ins = nc.tensor.matmul(bank[:, PJ[n], cols(t)], ctxT[:, cols(4 * n + t)],
                                       wl_sb[:, bass.ds(pair_row, 1), :].rearrange("p a c -> p (a c)"), start=True, stop=True)
            ins.then_inc(c_out, 1)

        def out_vector(v, pi, b, n):
            v.wait_ge(c_out, 2 * pi + n + 1)
            if n == 0:
                v.wait_ge(c_res, 2 * pi)
            xr = xres[:, bass.ds(b * T + 4 * n, 4), :]
            nc.vector.tensor_tensor(xr, bank[:, PJ[n], :].rearrange("p (t c) -> p t c", c=P), xr, ALU.add).then_inc(c_res, 1)

        def proj_hi(a, par, pr_i, k, bk):
            w = ws[par]
            a.wait_ge(c_proj, 6 * pr_i + k + 1)
            for h in range(2):
                r = rows(h)
                dst = qst[par][h][r, 0, cols(k % 2, HALF)] if k < 2 else kst[par][h][r, cols(k % 2, HALF)]
                bias = (w[r, BQ:BQ + 1] if k < 2 else w[r, BK:BK + 1]).bitcast(F32)
                nc.scalar.activation(dst, bank[r, bk, :], ACT.Identity, bias=bias).then_inc(c_hi, 1)

        def proj_lo(v, par, pr_i, k, bk):
            w = ws[par]
            if k >= 4:
                v.wait_ge(c_proj, 6 * pr_i + k + 1)
                nc.vector.tensor_tensor(vst[par][:, 4 * (k - 4):4 * (k - 3), :],
                                        bank[:, bk, :].rearrange("p (t c) -> p t c", c=P),
                                        w[:, BV:BV + P].bitcast(F32).unsqueeze(1).to_broadcast([P, 4, P]), ALU.add).then_inc(c_pev, 1)
                return
            for h in range(2):
                r, o = rows(h), rows(1 - h)
                v.wait_ge(c_hi, 8 * pr_i + 2 * k + h + 1)
                if k < 2:
                    hi, lo = qst[par][h][r, 0, cols(k, HALF)], qst[par][h][r, 1, cols(k, HALF)]
                    bias = w[r, BQ:BQ + 1].bitcast(F32)
                else:
                    hi, lo = kst[par][h][r, cols(k - 2, HALF)], kst[par][h][o, cols(k - 2, HALF)]
                    bias = w[r, BK:BK + 1].bitcast(F32)
                ins = nc.vector.scalar_tensor_tensor(out=lo, in0=bank[r, bk, :], scalar=bias, in1=hi.bitcast(F32),
                                                     op0=ALU.add, op1=ALU.subtract)
            ins.then_inc(c_pev, 1)

        def q_copy(sp, par, pr_i):
            for part in range(2):
                if part == 0:
                    hold(sp, c_hi, 8 * pr_i + 4)
                else:
                    hold(sp, c_pev, 6 * pr_i + 2)
                for h in range(2):
                    src = qst[par][h][rows(h), part, :].bitcast(F32)
                    dst = qst[par][h][rows(1 - h), part, :].bitcast(F32)
                    sp.dma_start(dst, src).then_inc(c_dup[h], 16)

        def scores(pe, par, j, g, pi, first=False):
            for h in range(2):
                if j == 0:
                    pe.wait_ge(c_dup[h], 32 * (pi + 1))
                if not first:
                    pe.wait_ge(c_exp, 2 * g + h - 1)
                for n in range(2):
                    o = bank[:, SC[h][n], :]
                    kk = kst[par][h][:, cols(j)]
                    nc.tensor.matmul(o, kk, qst[par][h][:, 0, cols(n, HALF)], start=True, stop=False)
                    ins = nc.tensor.matmul(o, kk, qst[par][h][:, 1, cols(n, HALF)], start=False, stop=True)
                ins.then_inc(c_qk, 1)

        def context(pe, j, g, pr_i):
            s = j % 2
            if j == 0:
                pe.wait_ge(c_ctx, 2 * pr_i)
            pe.wait_ge(c_vs, g + 1)
            for n in range(2):
                for h in range(2):
                    ins = nc.tensor.matmul(bank[rows(h), CX[n], :], vsc[s][:, rows(h)], prob[s][h][:, cols(n, HALF)],
                                           start=(j == 0), stop=(j == T - 1))
            ins.then_inc(c_av, 1)

        def score_max(v, g, s):
            for h in range(2):
                v.wait_ge(c_qk, 2 * g + h + 1)
                nc.vector.tensor_reduce(nmx[:, 2 * s + h:2 * s + h + 1], bank[:, SC[h][0]:SC[h][0] + 2, :],
                                        mybir.AxisListType.XY, ALU.max, negate=True).then_inc(c_max, 1)

        def score_exp(a, g, s):
            for h in range(2):
                a.wait_ge(c_max, 2 * g + h + 1)
                nc.scalar.activation(prob[s][h][:].rearrange("p (n c) -> p n c", c=HALF), bank[:, SC[h][0]:SC[h][0] + 2, :],
                                     ACT.Exp, bias=nmx[:, 2 * s + h:2 * s + h + 1],
                                     accum_out=zsum[:, 2 * s + h:2 * s + h + 1]).then_inc(c_exp, 1)

        def scale_v(v, step, par, j, g):
            s = j % 2
            v.wait_ge(c_exp, 2 * g + 2)
            step.then(nc.vector.reciprocal(zinv[:, 2 * s:2 * s + 2], zsum[:, 2 * s:2 * s + 2]))
            nc.vector.tensor_tensor(vsc[s][:].rearrange("p (h c) -> p h c", c=HD),
                                    vst[par][:, j, :].rearrange("p (h c) -> p h c", c=HD),
                                    zinv[:, 2 * s:2 * s + 2].unsqueeze(2).to_broadcast([P, 2, HD]), ALU.mult).then_inc(c_vs, 1)

        def steps_of(g0, pair0):
            for s in range(SPAN):
                yield s, s // T, s % T, g0 + s, pair0 + s // T

        def c_body_tensor(pe, g0, pair0, pair_row, first, last):
            for s, par, j, g, pi in steps_of(g0, pair0):
                if not (last and s == SPAN - 1):
                    if j == T - 1:
                        pe.wait_ge(c_pev, 6 * (pi + 1) + 4)
                        scores(pe, 1 - par, 0, g + 1, pi + 1)
                    else:
                        scores(pe, par, j + 1, g + 1, pi)
                if j < 6 and not (last and par == 1) and not (first and s < 2):
                    if j < 2:
                        pe.wait_ge(c_res, 2 * (pi - 2) + j + 1)
                    else:
                        pe.wait_ge(c_pev, 6 * (pi + 1) + j - 1)
                    project(pe, 1 - par, pi + 1, j, PJ[j % 2])
                if j >= 6 and not (first and par == 0):
                    out_tensor(pe, pi - 1, pair_row + par - 1, j - 6, last and par == 1)
                context(pe, j, g, pi)

        def ctx_evac(a, pi):
            a.wait_ge(c_av, T * (pi + 1))
            a.wait_ge(c_out, 2 * pi)
            for n in range(2):
                nc.scalar.activation(ctxT[:, cols(n, HALF)], bank[:, CX[n], :], ACT.Copy).then_inc(c_ctx, 1)

        def c_body_scalar(a, g0, pair0, first, last):
            for s, par, j, g, pi in steps_of(g0, pair0):
                if j == 0 and not (first and par == 0):
                    ctx_evac(a, pi - 1)
                if 1 <= j < 5 and not (last and par == 1):
                    proj_hi(a, 1 - par, pi + 1, j - 1, PJ[(j - 1) % 2])
                if not (last and s == SPAN - 1):
                    if j == 0 or (last and par == 1):
                        a.wait_ge(c_av, g)
                    score_exp(a, g + 1, (j + 1) % 2)

        def c_body_vector(v, step, g0, pair0, b, first, last, m=None, b_comb=None):
            for s, par, j, g, pi in steps_of(g0, pair0):
                if not (last and s == SPAN - 1):
                    score_max(v, g + 1, (j + 1) % 2)
                if j == 0 and not first:
                    out_vector(v, pi - 2, b, 1)
                if 1 <= j < 7 and not (last and par == 1):
                    proj_lo(v, 1 - par, pi + 1, j - 1, PJ[(j - 1) % 2])
                if j == T - 1 and not (first and par == 0):
                    out_vector(v, pi - 1, b, 0)
                if not (last and s == SPAN - 1):
                    v.wait_ge(c_av, g)
                    scale_v(v, step, (par + (j + 1) // T) % 2, (j + 1) % T, g + 1)
                if last and par == 1:
                    combine_tiles(v, step, m, b_comb, j // 4, [2 * (j % 4), 2 * (j % 4) + 1])

        MIDDLE = PAIRS // 2 - 2

        def c_tensor(pe, r, n):
            pe.wait_ge(ln_hi, n + 2)
            g0, p0 = PAIRS * T * r, PAIRS * r
            for k in range(6):
                if k == 3:
                    pe.wait_ge(f_ys, 3 * (r + B - 1))
                if k == 5:
                    pe.wait_ge(c_pev, 6 * p0 + 3)
                project(pe, 0, p0, k, FIRST_PJ[k], n)
            for k in range(2):
                project(pe, 1, p0 + 1, k, PJ[k])
            pe.wait_ge(c_pev, 6 * p0 + 4)
            scores(pe, 0, 0, g0, p0, first=True)
            pe.wait_ge(c_pev, 6 * p0 + 6)
            c_body_tensor(pe, g0, p0, 0, True, False)
            with pe.Fori(1, 1 + MIDDLE) as it:
                c_body_tensor(pe, g0 + SPAN * it, p0 + 2 * it, 2 * it, False, False)
            it = 1 + MIDDLE
            c_body_tensor(pe, g0 + SPAN * it, p0 + 2 * it, 2 * it, False, True)
            slots_tensor(pe, r + B - 1, THIRD_C)
            for h in range(2):
                out_tensor(pe, p0 + PAIRS - 1, PAIRS - 1, h, True)

        def c_scalar(a, r):
            g0, p0 = PAIRS * T * r, PAIRS * r
            for k in range(4):
                proj_hi(a, 0, p0, k, FIRST_PJ[k])
            score_exp(a, g0, 0)
            c_body_scalar(a, g0, p0, True, False)
            with a.Fori(1, 1 + MIDDLE) as it:
                c_body_scalar(a, g0 + SPAN * it, p0 + 2 * it, False, False)
            it = 1 + MIDDLE
            c_body_scalar(a, g0 + SPAN * it, p0 + 2 * it, False, True)
            ctx_evac(a, p0 + PAIRS - 1)

        def c_vector(v, step, r, n, b, b_comb):
            g0, p0 = PAIRS * T * r, PAIRS * r
            xT_lo_vector(v, n)
            for k in range(6):
                proj_lo(v, 0, p0, k, FIRST_PJ[k])
            score_max(v, g0, 0)
            bias_vector(v, step, n, b, bl_sb)
            scale_v(v, step, 0, 0, g0)
            begin = step.n
            c_body_vector(v, step, g0, p0, b, True, False)
            with v.Fori(1, 1 + MIDDLE) as it:
                step.n = begin + SPAN * it
                c_body_vector(v, step, g0 + SPAN * it, p0 + 2 * it, b, False, False)
            it = 1 + MIDDLE
            step.n = begin + SPAN * it
            c_body_vector(v, step, g0 + SPAN * it, p0 + 2 * it, b, False, True, r + B - 2, b_comb)
            out_vector(v, p0 + PAIRS - 2, b, 1)
            for h in range(2):
                out_vector(v, p0 + PAIRS - 1, b, h)
            hold(v, c_res, 2 * (p0 + PAIRS))

        def stage_pair(sp, pi, pair_row, par):
            hold(sp, c_pev, 6 * (pi - 1))
            sp.dma_start(ws[par][:].bitcast(F32), wpairs[bass.ds(pair_row * P, P), :]).then_inc(c_stage[par], 16)

        def c_sync(sp, r, pair_loads, last):
            p0 = PAIRS * r
            q_copy(sp, 0, p0)
            q_copy(sp, 1, p0 + 1)
            pair_loads()
            with sp.Fori(1, PAIRS // 2) as it:
                for par in range(2):
                    stage_pair(sp, p0 + 2 * it + par, 2 * it + par, par)
                    q_copy(sp, par, p0 + 2 * it + par)
            if not last:
                for par in range(2):
                    stage_pair(sp, p0 + PAIRS + par, par, par)
        stage_c.close()

        block = keep.enter_context(nc.Block())
        ITER_A = [0, 1]

        @block.sync
        def _(sp):
            xv = x.rearrange("(t p) c -> p t c", p=P)
            sp.dma_start(xres[:, 0:T, :], xv[:, 0:T, :]).then_inc(load_x0, 16)
            for dst, src in ((wa_sb[:, 0:P], win), (wa_sb[:, WG:WVA], wg), (wa_sb[:, WVA:], wv), (ca[:], cols_a)):
                sp.dma_start(dst, src).then_inc(load_a, 16)
            sp.dma_start(bout_sb[:], bout.partition_broadcast(P)).then_inc(load_a, 16)
            sp.dma_start(bv_sb[:], bv.partition_broadcast(P)).then_inc(load_a, 16)
            sp.dma_start(wout_sb[:], wout.rearrange("(e p) c -> p e c", p=P)).then_inc(load_a, 16)
            sp.dma_start(xres[:, T:, :], xv[:, T:, :]).then_inc(load_x, 16)
            split_loads(sp, 0)
            sp.dma_start(wr_sb[:], wr).then_inc(load_f, 16)
            sp.dma_start(bl_sb[:], bl.partition_broadcast(P)).then_inc(load_f, 16)
            sp.dma_start(b1_sb[:], b1).then_inc(load_f, 16)
            sp.dma_start(b2_sb[:], b2).then_inc(load_f, 16)
            sp.dma_start(wl_sb[:], wl).then_inc(load_f, 16)
            sp.wait_ge(zeroed, ZEROED)
            sp.dma_start(w1_sb[:], w1.rearrange("e p h -> p e h")).then_inc(load_f, 16)
            sp.dma_start(w2_sb[:], w2.rearrange("e (c p) n -> p e c n", p=P)).then_inc(load_f, 16)
            for b in range(B):
                split_stores(sp, b)
                if b < B - 1:
                    sp.wait_ge(w_stored, 32 * (b + 1))
                    split_loads(sp, b + 1)
                if b > 0:
                    load_slots(sp, b, b - 1)
                if b == B - 1:
                    sp.wait_ge(a_res, 2 * (B + 1))
                    sp.wait_ge(w_stored, 16 * PAIRS)
                    for par in range(2):
                        stage_pair(sp, PAIRS + par, par, par)
                if b > 0:
                    store_slots(sp, b, b - 1)
            with sp.Fori(0, B - 1) as b:
                c_sync(sp, b + 1, lambda: load_slots(sp, B + b, (b + B - 1) % B), False)
                store_slots(sp, B + b, (b + B - 1) % B)
            c_sync(sp, B, lambda: load_slots(sp, 2 * B - 1, B - 2), True)
            store_slots(sp, 2 * B - 1, B - 2)
            load_slots(sp, 2 * B, B - 1)
            for b in range(B):
                if b == B - 2:
                    store_slots(sp, 2 * B, B - 1)
                sp.wait_ge(f_comb, 2 * T * (B + b + 2))
                sp.dma_start(out[b * S:(b + 1) * S, :].rearrange("(t p) c -> p t c", p=P),
                             xres[:, b * T:(b + 1) * T, :]).then_inc(stored, 16)
            sp.wait_ge(stored, 16 * B)

        @block.gpsimd
        def _(p):
            step = Steps(p, pool_step)
            nc.gpsimd.memset(magic[:], 0x5f3759df).then_inc(magic_set, 1)
            step.done(nc.gpsimd.memset(xhat_r[:], 0.0))
            step.done(nc.gpsimd.memset(ident[:], 1.0))
            step.done(nc.gpsimd.memset(before[:], 1.0))
            step.done(nc.gpsimd.memset(ones[:], 1.0))
            step.done(nc.gpsimd.memset(m_quad[:], 0.0))
            step.done(nc.gpsimd.memset(m_lin[:], 0.0))
            step.done(nc.gpsimd.iota(rev[:], [[-1, E]], base=E, channel_multiplier=0, allow_small_or_imprecise_dtypes=True))
            step.done(nc.gpsimd.iota(rowbase[:], [[SLOTS, B], [CAP, E]], base=0, channel_multiplier=0,
                                     allow_small_or_imprecise_dtypes=True))
            step.wait()
            step.then(nc.gpsimd.affine_select(out=ident[:], in_=ident[:], compare_op=ALU.is_equal, fill=0.0, base=0,
                                              pattern=[[-1, P]], channel_multiplier=1))
            step.then(nc.gpsimd.affine_select(out=before[:], in_=before[:], compare_op=ALU.is_gt, fill=0.0, base=0,
                                              pattern=[[1, P]], channel_multiplier=-1))
            for g in range(P // GROUP):
                r = slice(g * GROUP, (g + 1) * GROUP)
                step.then(nc.gpsimd.memset(m_quad[r, r], float(INNER) ** -0.5))
                if g < P // GROUP - 1:
                    step.then(nc.gpsimd.memset(m_lin[r, (g + 1) * GROUP:P], 1.0))
                step.then(nc.gpsimd.affine_select(out=m_quad[r, r], in_=m_quad[r, r], compare_op=ALU.is_ge, fill=0.0, base=0,
                                                  pattern=[[1, GROUP]], channel_multiplier=-1))
            for s, count in per_row.items():
                p.sem_inc(s, count)
            p.sem_inc(consts, 1)
            p.wait_ge(load_a, 112)
            for slots, i in [(d, i) for d in (xslots, yslots) for i in range(B * ST // T)]:
                nc.gpsimd.dma_start(slots[i * S:(i + 1) * S, :].rearrange("(t p) c -> p t c", p=P), xhat_r[:]).then_inc(zeroed, 16)
            p.wait_ge(zeroed, ZEROED)
            for k in ITER_A:
                scatter(p, k + 1)
            begin = step.n
            with p.Fori(2, B) as b:
                step.n = begin + b - 2
                gather(p, step, b - 1, b - 2)
                scatter(p, b + 1)
            with p.Fori(0, B) as b:
                step.n = begin + B - 2 + b
                gather(p, step, B + b - 1, (b + 2) % B)
                scatter(p, B + b + 1)
            step.n = begin + 2 * B - 2
            gather(p, step, 2 * B - 1, B - 2)
            gather(p, step, 2 * B, B - 1)

        @block.scalar
        def _(a):
            a.wait_ge(consts, 1)
            xT_scalar(a, 1)
            a.wait_ge(load_a, 112)
            for k in ITER_A:
                a_scalar(a, k + 1)
                if k == 1:
                    a.wait_ge(load_f, 112)
                behind_scalar(a, k + 1, 2 * k + 2, THIRD_A, k > 0)
            with a.Fori(2, B) as b:
                a_scalar(a, b + 1)
                behind_scalar(a, b + 1, 2 * b + 2, THIRD_A)
            with a.Fori(0, B - 1) as b:
                c_scalar(a, b + 1)
                behind_scalar(a, B + b + 1, 2 * (B + b) + 2, THIRD_C)
            c_scalar(a, B)
            last_behind_scalar(a, 2 * B, 4 * B)
            slots_scalar(a, 2 * B, THIRD_A)
            experts_scalar(a, 2 * B, lambda e: None)

        @block.vector
        def _(v):
            v.wait_ge(magic_set, 1)
            v.wait_ge(load_x0, 16)
            step = Steps(v, dve_step)
            norms_vector(v, step, [(1, 0, xhat)])
            v.wait_ge(consts, 1)
            v.wait_ge(load_a, 112)
            step.then(nc.vector.tensor_copy(wa_hi[:], wa_sb[:]))
            nc.vector.tensor_tensor(wa_lo[:], wa_sb[:], wa_hi[:].bitcast(F32), ALU.subtract).then_inc(a_split, 1)
            for k in ITER_A:
                a_vector(v, step, k + 1, 2 * k + 1, k)
                if k == 0:
                    v.wait_ge(load_x, 16)
                    v.wait_ge(zeroed, ZEROED)
                norms_vector(v, step, [(2 * k + 2, k, xhat_r), (2 * k + 3, k + 1, xhat)], k + 1)
                route_vector(v, step, k + 1, k)
            begin, per = step.n, norm_steps(2) + 3 + 6 + ROUTE_STEPS + 1
            with v.Fori(2, B) as b:
                step.n = begin + (b - 2) * per
                a_vector(v, step, b + 1, 2 * b + 1, b)
                norms_vector(v, step, [(2 * b + 2, b, xhat_r), (2 * b + 3, (b + 1) % B, xhat)], b + 1)
                combine_vector(v, step, b - 1, b - 2)
                route_vector(v, step, b + 1, b)
            step.n = begin + (B - 2) * per
            begin, per = step.n, norm_steps(2) + 1 + PAIRS * T + ROUTE_STEPS + 1
            with v.Fori(0, B - 1) as b:
                step.n = begin + b * per
                c_vector(v, step, b + 1, 2 * (B + b) + 1, b, (b + 2) % B)
                norms_vector(v, step, [(2 * (B + b) + 2, b, xhat_r), (2 * (B + b) + 3, b + 1, xhat)], B + b + 1)
                route_vector(v, step, B + b + 1, b)
            step.n = begin + (B - 1) * per
            c_vector(v, step, B, 4 * B - 1, B - 1, 1)
            norms_vector(v, step, [(4 * B, B - 1, xhat_r)], 2 * B)
            route_vector(v, step, 2 * B, B - 1)
            combine_vector(v, step, 2 * B - 1, B - 2)
            combine_vector(v, step, 2 * B, B - 1)

        @block.tensor
        def _(pe):
            pe.wait_ge(consts, 1)
            ln_tensor(pe, 1, xhat, LN_MAIN)
            pe.wait_ge(a_split, 1)
            for k in ITER_A:
                a_tensor(pe, k + 1, 2 * k + 1, k > 0)
                if k == 0:
                    pe.wait_ge(load_f, 112)
                behind_tensor(pe, k + 1, 2 * k + 2, (a_res, 2 * (k + 2)), k > 0)
            with pe.Fori(2, B) as b:
                a_tensor(pe, b + 1, 2 * b + 1)
                behind_tensor(pe, b + 1, 2 * b + 2, (a_res, 2 * (b + 2)))
            with pe.Fori(0, B - 1) as b:
                c_tensor(pe, b + 1, 2 * (B + b) + 1)
                behind_tensor(pe, B + b + 1, 2 * (B + b) + 2, (c_res, 2 * PAIRS * (b + 2)))
            c_tensor(pe, B, 4 * B - 1)
            last_behind_tensor(pe, 2 * B, 4 * B, (c_res, 2 * PAIRS * (B + 1)))
            slots_tensor(pe, 2 * B, THIRD_A)
            experts_tensor(pe, 2 * B, lambda e: None)


ZEROED = 2 * 16 * (B * ST // T)



def kernel(**inputs):
    import numpy as np
    import concourse.bacc as bacc
    from concourse.bass_utils import run_bass_kernel_spmd

    def get(name):
        return np.asarray(inputs["L0_" + name])

    def attn(name):
        return get("attn_a_" + name)

    cols_a = np.stack([*attn("bg").reshape(EH, P), attn("bin_")] +
                      [attn(n) for n in ("g_qq", "b_qq", "g_qk", "b_qk", "g_lq", "b_lq", "g_lk", "b_lk")], axis=1)
    wqkv = np.stack([get(f"attn_b_{c}_w").reshape(PAIRS, P, P).transpose(2, 0, 1) for c in "qkv"], axis=2).reshape(P, PAIRS, 3 * P)
    bqk = np.stack([get(f"attn_b_{c}_b").reshape(PAIRS, P).T for c in "qk"], axis=2)
    arrays = {
        "x": attn("x").reshape(B * S, P), "wv": attn("Wv"), "bv": attn("bv"), "wg": attn("Wg"), "win": attn("Win"),
        "wout": attn("Wout"), "bout": attn("bout"), "cols_a": cols_a, "wr": get("ffn_Wr"), "w1": get("ffn_W1"),
        "b1": get("ffn_b1").reshape(E * HC, P).T, "w2": get("ffn_W2"), "b2": get("ffn_b2").T,
        "wqkv": wqkv, "bqk": bqk, "bvv": get("attn_b_v_b").reshape(PAIRS, P),
        "wl": get("attn_b_l_w").T.reshape(PAIRS, P, P).transpose(1, 0, 2), "bl": get("attn_b_l_b").reshape(P),
    }
    arrays = {n: np.ascontiguousarray(a) for n, a in arrays.items()}
    nc = bacc.Bacc("TRN2", target_bir_lowering=False, num_devices=1)
    args = {n: nc.dram_tensor("in_" + n, a.shape, mybir.dt.from_np(a.dtype), kind="ExternalInput").ap() for n, a in arrays.items()}
    result = nc.dram_tensor("out_x", (B * S, P), F32, kind="ExternalOutput").ap()
    bass_hybrid(nc, **args, out=result)
    r = run_bass_kernel_spmd(nc, [{"in_" + n: a for n, a in arrays.items()}], core_ids=[0])
    return r.results[0]["out_x"].reshape(B, S, P)
```
